# Optimizing a Trainium2 kernel written in Bass

```python
import numpy as np
import jax
import jax.numpy as jnp

def _softmax(x, axis=-1):
    return jax.nn.softmax(x, axis=axis)
def _gelu(x):
    return jax.nn.gelu(x, approximate=True)
def _silu(x):
    return jax.nn.silu(x)
def _sigmoid(x):
    return jax.nn.sigmoid(x)
def _layernorm(x, axis=-1, eps=1e-5):
    m = jnp.mean(x, axis=axis, keepdims=True)
    v = jnp.var(x, axis=axis, keepdims=True)
    return (x - m) / jnp.sqrt(v + eps)
def _scatter_add(tgt, idx, src, axis=0):
    return tgt.at[idx].add(src)
def _segment_sum(src, seg, n):
    return jax.ops.segment_sum(src, seg, n)

kernel_name = 'mk_adj_preln_d2_adj_512_219ef6'

def setup_inputs(seed: int = 0):
    np.random.seed(seed)
    _w = jnp.asarray
    def _rec_inputs():
        import jax
        import jax.numpy as jnp
        _gk = jax.random.key(seed)
        x = 7.22e-05 + 1 * jax.random.normal(jax.random.fold_in(_gk, 1), (128, 128, 512), jnp.float32)
        _w = (1.0 + jnp.arange(128, dtype=jnp.float32)) ** -0.5
        _w = _w / _w.mean()
        _pij = jnp.clip(0.0625 * _w[:, None] * _w[None, :], 0.0, 1.0)
        _a = jax.random.uniform(jax.random.fold_in(_gk, 2), (128, 128, 128)) < _pij
        _a = jnp.logical_or(_a, jnp.swapaxes(_a, -1, -2))
        _a = jnp.logical_or(_a, jnp.eye(128, dtype=bool))
        _af = _a.astype(jnp.float32)
        _af = _af * jax.random.uniform(jax.random.fold_in(_gk, 3), (128, 128, 128), jnp.float32, 0.05, 1)
        adj = _af
        return x, adj
    x, adj = _rec_inputs()
    def _L0_gnn_setup():
        import jax, jax.numpy as jnp
        import numpy as np
        B, N, F_IN, F_OUT = (8, 2048, 512, 512)
        key = jax.random.key(seed)
        k1, k2, k3, k4 = jax.random.split(key, 4)
        X = jax.random.normal(k1, (B, N, F_IN), dtype=jnp.float32)
        A = jax.random.uniform(k2, (B, N, N), dtype=jnp.float32)
        bound = 1.0 / np.sqrt(F_IN)
        W = jax.random.uniform(k3, (F_IN, F_OUT), dtype=jnp.float32, minval=-bound, maxval=bound)
        b = jax.random.uniform(k4, (F_OUT,), dtype=jnp.float32, minval=-bound, maxval=bound)
        return {'X': X, 'A': A, 'W': W, 'b': b}
    _L0_gnn_all = _L0_gnn_setup()
    _L0_gnn_in = {k: v for k, v in _L0_gnn_all.items() if k in ('W', 'b', )}
    del _L0_gnn_all

    def _L1_gnn_setup():
        import jax, jax.numpy as jnp
        import numpy as np
        EPS_LN = 1e-05

        def hypergraph_conv(x, adj, W, b):
            N, C, _ = adj.shape
            H = (adj != 0).astype(x.dtype)
            w = adj.reshape(N, -1)[:, :C]
            xw = jnp.einsum('ncd,hd->nch', x, W)
            Dn = jnp.einsum('nce,ne->nc', H, w)
            Dn = jnp.where(Dn > 0, 1.0 / Dn, 0.0)
            Be = H.sum(axis=1)
            Be = jnp.where(Be > 0, 1.0 / Be, 0.0)
            m = Be[:, :, None] * jnp.einsum('nce,nch->neh', H, xw)
            out = Dn[:, :, None] * jnp.einsum('nce,neh->nch', H, m)
            return out + b

        def layer_norm(x, g, b):
            mu = jnp.mean(x, axis=-1, keepdims=True)
            var = jnp.var(x, axis=-1, keepdims=True)
            return (x - mu) * jax.lax.rsqrt(var + EPS_LN) * g + b
        key = jax.random.key(seed)
        ks = jax.random.split(key, 4)
        N, C, Din, Dh, Dout = (16, 1024, 512, 1024, 512)
        x = jax.random.normal(ks[0], (N, C, Din), dtype=jnp.float32)
        adj = jax.random.uniform(ks[1], (N, C, C), dtype=jnp.float32, minval=0.1, maxval=1.0)
        W1 = jax.random.normal(ks[2], (Dh, Din), dtype=jnp.float32) * (1.0 / np.sqrt(Din))
        b1 = jnp.zeros((Dh,), dtype=jnp.float32)
        gamma = jnp.ones((Dh,), dtype=jnp.float32)
        beta = jnp.zeros((Dh,), dtype=jnp.float32)
        W2 = jax.random.normal(ks[3], (Dout, Dh), dtype=jnp.float32) * (1.0 / np.sqrt(Dh))
        b2 = jnp.zeros((Dout,), dtype=jnp.float32)
        return {'x': x, 'adj': adj, 'W1': W1, 'b1': b1, 'gamma': gamma, 'beta': beta, 'W2': W2, 'b2': b2}
    _L1_gnn_all = _L1_gnn_setup()
    _L1_gnn_in = {k: v for k, v in _L1_gnn_all.items() if k in ('W1', 'b1', 'gamma', 'beta', 'W2', 'b2', )}
    del _L1_gnn_all

    return {
        "x": x,
        "adj": adj,
        "L0_gnn_W": _L0_gnn_in["W"],
        "L0_gnn_b": _L0_gnn_in["b"],
        "L1_gnn_W1": _L1_gnn_in["W1"],
        "L1_gnn_b1": _L1_gnn_in["b1"],
        "L1_gnn_gamma": _L1_gnn_in["gamma"],
        "L1_gnn_beta": _L1_gnn_in["beta"],
        "L1_gnn_W2": _L1_gnn_in["W2"],
        "L1_gnn_b2": _L1_gnn_in["b2"],
    }

def reference(x, adj, L0_gnn_W, L0_gnn_b, L1_gnn_W1, L1_gnn_b1, L1_gnn_gamma, L1_gnn_beta, L1_gnn_W2, L1_gnn_b2):
    import jax
    import jax.numpy as jnp
    def _L0_gnn_ref(X, A, W, b):
        import jax, jax.numpy as jnp
        import numpy as np
        B, N, F_IN, F_OUT = (8, 2048, 512, 512)
        A_hat = A + jnp.eye(A.shape[-1], dtype=A.dtype)
        d_inv_sqrt = A_hat.sum(axis=-1) ** (-0.5)
        L = A_hat * d_inv_sqrt[:, :, None] * d_inv_sqrt[:, None, :]
        x = X @ W + b
        return jnp.einsum('bij,bjf->bif', L, x)

    def _L1_gnn_ref(x, adj, W1, b1, gamma, beta, W2, b2):
        import jax, jax.numpy as jnp
        import numpy as np
        EPS_LN = 1e-05

        def hypergraph_conv(x, adj, W, b):
            N, C, _ = adj.shape
            H = (adj != 0).astype(x.dtype)
            w = adj.reshape(N, -1)[:, :C]
            xw = jnp.einsum('ncd,hd->nch', x, W)
            Dn = jnp.einsum('nce,ne->nc', H, w)
            Dn = jnp.where(Dn > 0, 1.0 / Dn, 0.0)
            Be = H.sum(axis=1)
            Be = jnp.where(Be > 0, 1.0 / Be, 0.0)
            m = Be[:, :, None] * jnp.einsum('nce,nch->neh', H, xw)
            out = Dn[:, :, None] * jnp.einsum('nce,neh->nch', H, m)
            return out + b

        def layer_norm(x, g, b):
            mu = jnp.mean(x, axis=-1, keepdims=True)
            var = jnp.var(x, axis=-1, keepdims=True)
            return (x - mu) * jax.lax.rsqrt(var + EPS_LN) * g + b
        h = jax.nn.relu(hypergraph_conv(x, adj, W1, b1))
        h = layer_norm(h, gamma, beta)
        y = hypergraph_conv(h, adj, W2, b2)
        return y + x

    h = jnp.maximum(_layernorm(x, axis=-1), 0.0)
    x = x + _L0_gnn_ref(h, adj, L0_gnn_W, L0_gnn_b)
    h = jnp.maximum(_layernorm(x, axis=-1), 0.0)
    x = x + _L1_gnn_ref(h, adj, L1_gnn_W1, L1_gnn_b1, L1_gnn_gamma, L1_gnn_beta, L1_gnn_W2, L1_gnn_b2)
    return x


_drawn_inputs = setup_inputs


def setup_inputs(seed=0):
    import zlib

    import numpy as np

    out = dict(_drawn_inputs(seed))
    spreads = {'L1_gnn_b1': (0.0, 0.1),
     'L1_gnn_gamma': (1.0, 0.2),
     'L1_gnn_beta': (0.0, 0.1),
     'L1_gnn_b2': (0.0, 0.322)}
    factors = {}
    for name, (base, spread) in spreads.items():
        noise = np.random.default_rng([zlib.crc32(name.encode()), seed]).standard_normal(out[name].shape)
        drawn = base * np.exp(spread * noise) if base else spread * noise
        out[name] = jnp.asarray(drawn.astype(out[name].dtype))
    for name, factor in factors.items():
        out[name] = (out[name] * factor).astype(out[name].dtype)
    return out
```

```python
import concourse.bass as bass
from concourse import mybir
from contextlib import ExitStack


def bass_adjacency_prenorm_two_layer_gnn_kernel(
    nc: bass.Bass,
    x: bass.AP,
    adj: bass.AP,
    W: bass.AP,
    b: bass.AP,
    W1T: bass.AP,
    b1: bass.AP,
    gamma: bass.AP,
    beta: bass.AP,
    W2T: bass.AP,
    b2: bass.AP,
    out: bass.AP,
):
    F32, F32R, F16 = mybir.dt.float32, mybir.dt.float32r, mybir.dt.float16
    ALU = mybir.AluOpType
    ACT = mybir.ActivationFunctionType
    AX = mybir.AxisListType
    ENG = mybir.EngineType

    NG, N, DIN = x.shape
    DH = W1T.shape[1]
    CH = 512
    KI, KH = DIN // 128, DH // 128
    NCH = DH // CH
    EPS = 1e-5
    P_SCALE = 2.0 ** 8
    X_SCALE = 2.0 ** 11
    H_SCALE = 2.0 ** 10
    DN1_SCALE = 1.0 / (P_SCALE * X_SCALE)
    DN2_SCALE = 1.0 / (P_SCALE * H_SCALE)
    TINY = 1.1754944e-38

    LOOP_FROM = 5
    LOOP_TO = NG - 1
    assert (LOOP_TO - LOOP_FROM) % 2 == 0 and LOOP_TO > LOOP_FROM
    ORDER = list(range(-1, LOOP_FROM)), list(range(LOOP_TO, NG + 3))

    ctx = ExitStack()
    with ctx:
        def sb(name, shape, dt=F32):
            return ctx.enter_context(nc.sbuf_tensor(name, shape, dt))

        def sem(name):
            return ctx.enter_context(nc.semaphore(name))

        stage = sb("stage", [128, 2, 4096])
        w0h, w0l = sb("w0h", [128, KI, DIN], F32R), sb("w0l", [128, KI, DIN], F32R)
        w1h, w1l = sb("w1h", [128, KI, DH], F32R), sb("w1l", [128, KI, DH], F32R)
        w2h, w2l = sb("w2h", [128, KH, DIN], F32R), sb("w2l", [128, KH, DIN], F32R)
        gam, bet = sb("gam", [128, KH]), sb("bet", [128, KH])
        bet_wide = sb("bet_wide", [128, KH, 128])
        b_all, b1_all, b2_all = sb("b_all", [128, DIN]), sb("b1_all", [128, DH]), sb("b2_all", [128, DIN])
        v_all = sb("v_all", [128, DIN])
        ident = sb("ident", [128, 128])
        neg_half = sb("neg_half", [128, 2])
        neg_one = sb("neg_one", [128, 1])
        eps_one = sb("eps_one", [128, 2])

        x_t = sb("x_t", [128, 2, DIN])
        adj_t = sb("adj_t", [128, 2, N])
        wrow_t = sb("wrow_t", [128, 2, N])
        hit = sb("hit", [128, N])
        ahat_T = sb("ahat_T", [128, 2, N])
        H_T = sb("H_T", [128, 2, N], F16)
        HB_hi, HB_lo = sb("HB_hi", [128, 2, N], F16), sb("HB_lo", [128, 2, N], F16)
        P_hi, P_lo = sb("P_hi", [128, 2, N], F16), sb("P_lo", [128, 2, N], F16)
        h0 = sb("h0", [128, 2, DIN])
        t0h, t0l = sb("t0h", [128, DIN], F32R), sb("t0l", [128, DIN], F32R)
        t1h, t1l = sb("t1h", [128, DIN], F32R), sb("t1l", [128, DIN], F32R)
        t2h, t2l = sb("t2h", [128, DH], F32R), sb("t2l", [128, DH], F32R)
        base0, scr0 = sb("base0", [128, DIN]), sb("scr0", [128, DIN])
        x1 = sb("x1", [128, 2, DIN])
        xh = sb("xh", [128, 2, DIN])
        xh_hi, xh_lo = sb("xh_hi", [128, DIN], F16), sb("xh_lo", [128, DIN], F16)
        z, h = sb("z", [128, DH]), sb("h", [128, DH])
        hn = sb("hn", [128, DH])
        hn_hi, hn_lo = sb("hn_hi", [128, DH], F16), sb("hn_lo", [128, DH], F16)
        sum2, scr2 = sb("sum2", [128, DIN]), sb("scr2", [128, DIN])
        base2 = sb("base2", [128, 2, DIN])
        out_t = sb("out_t", [128, 2, DIN])
        raw0, raw1, raw2 = sb("raw0", [128, 6]), sb("raw1", [128, 6]), sb("raw2", [128, NCH, 6])
        st0 = sb("st0", [128, 2, 3])
        st1, st2 = sb("st1", [128, 2]), sb("st2", [128, 2])
        pw0, pw1, pw2 = sb("pw0", [128, 2]), sb("pw1", [128, 1]), sb("pw2", [128, 1])
        rd0 = sb("rd0", [128, 2, 2])
        sc0, sc1, sc2 = sb("sc0", [128, 2, 2]), sb("sc1", [128, 2]), sb("sc2", [128, 2])
        nm0, nm1, nm2 = sb("nm0", [128, 1]), sb("nm1", [128, 1]), sb("nm2", [128, 1])
        q_dn = sb("q_dn", [128, 1])
        s_in = sb("s_in", [128, 1])
        deg, cnt = sb("deg", [128, 2]), sb("cnt", [128, 2])
        inv_b, inv_t = sb("inv_b", [128, 1]), sb("inv_t", [128, 1])
        inv_d, inv_r = sb("inv_d", [128, 1]), sb("inv_r", [128, 1])
        dn1, dn2 = sb("dn1", [128, 2]), sb("dn2", [128, 2])
        q = sb("q", [128, 2])

        def bank(name, n=1):
            return ctx.enter_context(nc.psum_tensor(name, [128, n * CH], F32))

        ps_t2 = bank("ps_t2", 2)
        ps_y1 = bank("ps_y1", 2)
        ps_t1 = bank("ps_t1")
        ps_t0 = bank("ps_t0")
        ps_at = bank("ps_at")
        ps_p = bank("ps_p")
        ps_y0 = ps_t1
        ps_y2 = ps_t2[:, 0:CH]
        AT = ps_at[:, 0:N]
        ROW = ps_at[:, N:N + 1]
        PP = ps_p[:, 0:N]

        s_const = sem("consts_built")
        s_small = sem("small_params_loaded")
        s_stage = [sem("stage_loaded_0"), sem("stage_loaded_1")]
        s_whi = sem("weights_hi_split")
        s_wlo = sem("weights_lo_split")
        s_scaled = sem("w2_gamma_scaled")
        s_betw = sem("beta_widened")
        s_vps = sem("v_in_psum")
        s_v = sem("v_ready")
        s_x = [sem("x_loaded_0"), sem("x_loaded_1")]
        s_adj = [sem("adj_loaded_0"), sem("adj_loaded_1")]
        s_st = [sem("out_stored_0"), sem("out_stored_1")]
        s_zero = sem("ident_zeroed")
        s_at, s_ahat, s_ht = sem("adjT_in_psum"), sem("ahatT_ready"), sem("HT_parts_ready")
        s_stat0, s_ln0, s_h0 = sem("stats0_ready"), sem("ln0_scalars_ready"), sem("h0_ready")
        s_t0, s_t0h, s_t0l = sem("t0_in_psum"), sem("t0_hi_ready"), sem("t0_lo_ready")
        s_s, s_base0 = sem("bias0_factor_ready"), sem("base0_ready")
        s_y0, s_x1 = sem("y0_in_psum"), sem("x1_ready")
        s_stat1, s_ln1, s_xh = sem("stats1_ready"), sem("ln1_scalars_ready"), sem("xh_ready")
        s_xhh, s_xhl = sem("xh_hi_ready"), sem("xh_lo_ready")
        s_p, s_ph, s_pl = sem("P_in_psum"), sem("P_hi_ready"), sem("P_lo_ready")
        s_t1, s_t1h, s_t1l = sem("t1_in_psum"), sem("t1_hi_ready"), sem("t1_lo_ready")
        s_y1 = [sem(f"y1_chunk{c}_in_psum") for c in range(NCH)]
        s_z = [sem(f"z_chunk{c}_ready") for c in range(NCH)]
        s_h = [sem(f"h_chunk{c}_ready") for c in range(NCH)]
        s_stat2, s_ln2, s_hn = sem("stats2_ready"), sem("ln2_scalars_ready"), sem("hn_ready")
        s_hnh, s_hnl = sem("hn_hi_ready"), sem("hn_lo_ready")
        s_dn2, s_base2 = sem("dn2_ready"), sem("base2_ready")
        s_t2, s_t2h, s_t2l = sem("t2_in_psum"), sem("t2_hi_ready"), sem("t2_lo_ready")
        s_y2, s_out = sem("y2_in_psum"), sem("out_ready")
        s_raw0, s_raw1, s_raw2 = sem("bn_raw0_ready"), sem("bn_raw1_ready"), sem("bn_raw2_ready")
        s_deg, s_degsafe, s_deginv, s_dn1 = sem("deg_ready"), sem("deg_safe"), sem("deg_inverted"), sem("dn1_ready")
        s_cnt, s_cntsafe, s_cntinv, s_hbhi = sem("cnt_ready"), sem("cnt_safe"), sem("cnt_inverted"), sem("HB_hi_ready")
        s_pscr0 = sem("bias0_rows_ready")
        s_pe0, s_pp0, s_pr0 = sem("ln0_var_eps"), sem("ln0_rstd_and_D"), sem("ln0_rstd_D_product")
        s_pe1, s_pp1 = sem("ln1_var_eps"), sem("ln1_rstd")
        s_qdn = sem("q_dn_product")
        s_pe2, s_pp2 = sem("ln2_var_eps"), sem("ln2_rstd")
        s_psum2a, s_psum2b, s_psum2c = sem("x1_plus_xh"), sem("x1_xh_b2_sum"), sem("beta_rows_ready")

        def live(g, i):
            return not isinstance(i, int) or 0 <= g < NG

        def wait(eng, s, i, g):
            if not isinstance(i, int) or g >= 0:
                eng.wait_ge(s, i + (g + 1))

        def wait_dma(eng, pair, i, g, each=16):
            if not isinstance(i, int) or g >= 0:
                eng.wait_ge(pair[g % 2], i * (each // 2) + each * (g // 2 + 1))

        def every_step(eng_type, step):
            for k in ORDER[0]:
                step(0, k)
            with nc.Fori(0, LOOP_TO - LOOP_FROM, 2, engines=(eng_type,), hint_back_edge=True) as i:
                step(i, LOOP_FROM)
                step(i, LOOP_FROM + 1)
            for k in ORDER[1]:
                step(0, k)

        block = ctx.enter_context(nc.Block())

        @block.sync
        def _(sp):
            def load_adj(i, g):
                n = g % 2
                at = bass.ds(i + g, 1)
                sp.dma_start(adj_t[:, n, :], adj[at, :, :].rearrange("g n e -> n (g e)")).then_inc(s_adj[n], 16)
                sp.dma_start(wrow_t[:, n, :], adj[at, 0, :].to_broadcast([128, N])).then_inc(s_adj[n], 16)

            def load_x(i, g):
                sp.dma_start(x_t[:, g % 2, :], x[bass.ds(i + g, 1), :, :].rearrange("g n f -> n (g f)"))\
                  .then_inc(s_x[g % 2], 16)

            load_adj(0, 0)
            load_x(0, 0)
            sp.dma_start(stage[:, 0, 0:KI * DIN].rearrange("p (t n) -> p t n", t=KI),
                         W.rearrange("(t p) n -> p t n", p=128)).then_inc(s_stage[0], 16)
            sp.dma_start(stage[:, 1, :].rearrange("p (t n) -> p t n", t=KI),
                         W1T.rearrange("(t p) n -> p t n", p=128)).then_inc(s_stage[1], 16)
            for row, src in ((b_all, b), (b1_all, b1), (b2_all, b2)):
                sp.dma_start(row[:, :], src.rearrange("(a n) -> a n", a=1).to_broadcast([128, src.shape[0]]))\
                  .then_inc(s_small, 16)
            for col, src in ((gam, gamma), (bet, beta)):
                sp.dma_start(col[:, :], src).then_inc(s_small, 16)
            load_adj(0, 1)
            load_x(0, 1)
            sp.wait_ge(s_whi, 1)
            sp.wait_ge(s_wlo, 1)
            sp.dma_start(stage[:, 0, :].rearrange("p (t n) -> p t n", t=KH),
                         W2T.rearrange("(t p) n -> p t n", p=128)).then_inc(s_stage[0], 16)

            def step(i, k):
                g, o = k + 2, k - 3
                if live(o, i):
                    wait(sp, s_out, i, o)
                    sp.dma_start(out[bass.ds(i + o, 1), :, :].rearrange("g n f -> n (g f)"), out_t[:, o % 2, :])\
                      .then_inc(s_st[o % 2], 16)
                if isinstance(i, int) and not 2 <= g < NG:
                    return
                wait(sp, s_stat0, i, g - 2)
                wait(sp, s_at, i, g - 2)
                load_adj(i, g)
                wait(sp, s_h0, i, g - 2)
                wait(sp, s_base0, i, g - 2)
                load_x(i, g)

            for k in ORDER[0]:
                step(0, k)
            with nc.Fori(0, LOOP_TO - LOOP_FROM - 2, 2, engines=(ENG.SP,), hint_back_edge=True) as i:
                step(i, LOOP_FROM)
                step(i, LOOP_FROM + 1)
            for k in [LOOP_TO - 2, LOOP_TO - 1] + ORDER[1]:
                step(0, k)
            for g in (NG - 2, NG - 1):
                wait_dma(sp, s_st, 0, g)

        @block.tensor
        def _(pe):
            def thin(ps, lhs, rhs):
                (lh, ll), (rh, rl) = lhs, rhs
                pe.matmul(ps, lh, rh, start=True, stop=False)
                pe.matmul(ps, lh, rl, start=False, stop=False)
                return pe.matmul(ps, ll, rh, start=False, stop=True)

            def with_weights(ps, t_hi, t_lo, w_hi, w_lo, blocks, cols):
                for n, (t, w) in enumerate(((t_hi, w_hi), (t_hi, w_lo), (t_lo, w_hi))):
                    for j in range(blocks):
                        mm = pe.matmul(ps, t[:, j * 128:(j + 1) * 128], w[:, j, cols],
                                       start=(n == 0 and j == 0), stop=(n == 2 and j == blocks - 1))
                return mm

            def beta_row():
                pe.wait_ge(s_betw, 1)
                pe.wait_ge(s_stage[0], 32)
                raw = stage[:, 0, :].rearrange("p (t n) -> p t n", t=KH)
                for j in range(KH):
                    mm = pe.matmul(ps_y2, bet_wide[:, j, :], raw[:, j, :], start=(j == 0), stop=(j == KH - 1))
                mm.then_inc(s_vps, 1)

            def step(i, k):
                p, a, c1, c2, o = k + 1, k, k - 1, k - 2, k - 3
                if isinstance(i, int) and c1 == 0:
                    beta_row()
                if live(c1, i):
                    m = c1 % 2
                    wait(pe, s_xhh, i, c1)
                    wait(pe, s_xhl, i, c1)
                    wait(pe, s_pl, i, c1)
                    wait(pe, s_x1, i, c1)
                    for j in range(KI):
                        f = slice(j * 128, (j + 1) * 128)
                        mm = thin(ps_t1[:, f], (xh_hi[:, f], xh_lo[:, f]), (P_hi[:, m, :], P_lo[:, m, :]))
                    mm.then_inc(s_t1, 1)
                if live(a, i):
                    m = a % 2
                    wait(pe, s_ln0, i, a)
                    wait(pe, s_ahat, i, a)
                    wait(pe, s_ht, i, a)
                    wait(pe, s_h0, i, a)
                    wait(pe, s_t0l, i, a - 1)
                    pe.matmul(ROW, ahat_T[:, m, :], rd0[:, m, 1:2], start=True, stop=True)
                    for j in range(KI):
                        f = slice(j * 128, (j + 1) * 128)
                        mm = pe.matmul(ps_t0[:, f], h0[:, m, f], ahat_T[:, m, :], start=True, stop=True)
                    mm.then_inc(s_t0, 1)
                if live(c2, i):
                    m = c2 % 2
                    wait(pe, s_hnh, i, c2)
                    wait(pe, s_hnl, i, c2)
                    wait(pe, s_out, i, o)
                    wait(pe, s_t2l, i, c2 - 1)
                    if isinstance(i, int) and c2 == 0:
                        pe.wait_ge(s_v, 1)
                    for j in range(KH):
                        f = slice(j * 128, (j + 1) * 128)
                        mm = thin(ps_t2[:, f], (hn_hi[:, f], hn_lo[:, f]), (P_hi[:, m, :], P_lo[:, m, :]))
                    mm.then_inc(s_t2, 1)
                if live(c1, i):
                    if isinstance(i, int) and c1 == 0:
                        pe.wait_ge(s_wlo, 2)
                        pe.wait_ge(s_whi, 2)
                    wait(pe, s_t1h, i, c1)
                    wait(pe, s_t1l, i, c1)
                    for c in range(NCH):
                        wait(pe, s_z[c], i, c1 - 1)
                        cols = slice(c * CH, (c + 1) * CH)
                        with_weights(ps_y1[:, cols], t1h, t1l, w1h, w1l, KI, cols).then_inc(s_y1[c], 1)
                if live(p, i):
                    wait_dma(pe, s_adj, i, p, 32)
                    if isinstance(i, int) and p == 0:
                        pe.wait_ge(s_const, 1)
                    wait(pe, s_s, i, a)
                    pe.transpose(AT, adj_t[:, p % 2, :], ident[:, :]).then_inc(s_at, 1)
                if live(a, i):
                    if isinstance(i, int) and a == 0:
                        pe.wait_ge(s_wlo, 1)
                        pe.wait_ge(s_whi, 1)
                    wait(pe, s_t0h, i, a)
                    wait(pe, s_t0l, i, a)
                    with_weights(ps_y0[:, :], t0h, t0l, w0h, w0l, KI, slice(0, DIN)).then_inc(s_y0, 1)
                    m = a % 2
                    wait(pe, s_pl, i, a - 1)
                    pe.matmul(PP, HB_hi[:, m, :], H_T[:, m, :], start=True, stop=False)
                    pe.matmul(PP, HB_lo[:, m, :], H_T[:, m, :], start=False, stop=True).then_inc(s_p, 1)
                if live(c2, i):
                    if isinstance(i, int) and c2 == 0:
                        pe.wait_ge(s_wlo, 3)
                        pe.wait_ge(s_whi, 3)
                    wait(pe, s_t2h, i, c2)
                    wait(pe, s_t2l, i, c2)
                    with_weights(ps_y2, t2h, t2l, w2h, w2l, KH, slice(0, DIN)).then_inc(s_y2, 1)

            every_step(ENG.PE, step)

        @block.scalar
        def _(act):
            def split_hi(n, w_hi, raw):
                act.activation(w_hi, raw, ACT.Copy).then_inc(s_whi, 1)

            act.wait_ge(s_stage[0], 16)
            split_hi(0, w0h[:, :, :], stage[:, 0, 0:KI * DIN].rearrange("p (t n) -> p t n", t=KI))
            act.wait_ge(s_stage[1], 16)
            split_hi(1, w1h[:, :, :], stage[:, 1, :].rearrange("p (t n) -> p t n", t=KI))

            def step(i, k):
                p, a, c1, c2 = k + 1, k, k - 1, k - 2
                if isinstance(i, int) and c1 == 0:
                    act.wait_ge(s_scaled, 1)
                    split_hi(2, w2h[:, :, :], stage[:, 1, :].rearrange("p (t n) -> p t n", t=KH))
                if live(c1, i):
                    wait(act, s_t1, i, c1)
                    wait(act, s_y1[NCH - 1], i, c1 - 1)
                    act.activation(t1h[:, :], ps_t1[:, :], ACT.Copy).then_inc(s_t1h, 1)
                if live(a, i):
                    wait(act, s_t0, i, a)
                    wait(act, s_y0, i, a - 1)
                    act.activation(t0h[:, :], ps_t0[:, :], ACT.Copy).then_inc(s_t0h, 1)
                if live(c2, i):
                    wait(act, s_t2, i, c2)
                    wait(act, s_y2, i, c2 - 1)
                    act.activation(t2h[:, :], ps_t2[:, :], ACT.Copy).then_inc(s_t2h, 1)
                if live(p, i):
                    m = p % 2
                    wait(act, s_ln0, i, p)
                    wait_dma(act, s_x, i, p)
                    wait(act, s_t0, i, p - 2)
                    act.activation(h0[:, m, :], x_t[:, m, :], ACT.Relu, bias=sc0[:, m, 1:2],
                                   scale=sc0[:, m, 0:1]).then_inc(s_h0, 1)
                if live(c1, i):
                    for c in range(NCH):
                        cols = slice(c * CH, (c + 1) * CH)
                        wait(act, s_z[c], i, c1)
                        if c == 0:
                            wait(act, s_stat2, i, c1 - 1)
                            wait(act, s_hn, i, c1 - 1)
                        act.activation(h[:, cols], z[:, cols], ACT.Relu).then_inc(s_h[c], 1)
                if live(a, i):
                    m = a % 2
                    wait(act, s_p, i, a)
                    wait(act, s_t2, i, a - 2)
                    wait(act, s_base2, i, a - 2)
                    act.activation(P_hi[:, m, :], PP, ACT.Copy, accum_out=q[:, m:m + 1]).then_inc(s_ph, 1)
                if live(c1, i):
                    wait(act, s_ln2, i, c1)
                    wait(act, s_h[NCH - 1], i, c1)
                    wait(act, s_hnl, i, c1 - 1)
                    wait(act, s_hnh, i, c1 - 1)
                    act.activation(hn[:, :], h[:, :], ACT.Identity, bias=sc2[:, 1:2],
                                   scale=sc2[:, 0:1]).then_inc(s_hn, 1)
                if live(a, i):
                    m = a % 2
                    wait(act, s_ln1, i, a)
                    wait(act, s_base2, i, a - 2)
                    wait(act, s_xhl, i, a - 2)
                    act.activation(xh[:, m, :], x1[:, m, :], ACT.Relu, bias=sc1[:, 1:2],
                                   scale=sc1[:, 0:1]).then_inc(s_xh, 1)
                    wait(act, s_xh, i, a)
                    wait(act, s_t1, i, a - 1)
                    act.activation(xh_hi[:, :], xh[:, m, :], ACT.Copy, scale=X_SCALE).then_inc(s_xhh, 1)
                if live(c1, i):
                    wait(act, s_hn, i, c1)
                    wait(act, s_t2, i, c1 - 1)
                    act.activation(hn_hi[:, :], hn[:, :], ACT.Copy, scale=H_SCALE).then_inc(s_hnh, 1)

            every_step(ENG.Activation, step)

        @block.vector
        def _(dve):
            def split_lo(n, w_lo, raw, w_hi):
                dve.wait_ge(s_whi, n + 1)
                dve.tensor_tensor(w_lo, raw, w_hi.bitcast(F32), ALU.subtract).then_inc(s_wlo, 1)

            dve.wait_ge(s_stage[0], 16)
            split_lo(0, w0l[:, :, :], stage[:, 0, 0:KI * DIN].rearrange("p (t n) -> p t n", t=KI), w0h[:, :, :])
            dve.wait_ge(s_stage[1], 16)
            split_lo(1, w1l[:, :, :], stage[:, 1, :].rearrange("p (t n) -> p t n", t=KI), w1h[:, :, :])
            dve.wait_ge(s_small, 5 * 16)
            dve.tensor_copy(bet_wide[:, :, :], bet[:, :].unsqueeze(2).to_broadcast([128, KH, 128]))\
               .then_inc(s_betw, 1)
            dve.wait_ge(s_stage[0], 32)
            dve.wait_ge(s_wlo, 2)
            for j in range(KH):
                last = dve.tensor_scalar(stage[:, 1, j * DIN:(j + 1) * DIN], stage[:, 0, j * DIN:(j + 1) * DIN],
                                         gam[:, j:j + 1], None, ALU.mult)
            last.then_inc(s_scaled, 1)

            def tail_of_weights():
                dve.wait_ge(s_scaled, 1)
                raw = stage[:, 1, :].rearrange("p (t n) -> p t n", t=KH)
                split_lo(2, w2l[:, :, :], raw, w2h[:, :, :])
                dve.wait_ge(s_vps, 1)
                dve.tensor_scalar(v_all[:, :], ps_y2, H_SCALE, None, ALU.mult).then_inc(s_v, 1)

            def step(i, k):
                p, a, c1, c2, o = k + 1, k, k - 1, k - 2, k - 3
                if live(o, i):
                    m = o % 2
                    wait(dve, s_y2, i, o)
                    wait(dve, s_base2, i, o)
                    wait(dve, s_dn2, i, o)
                    wait_dma(dve, s_st, i, o - 2)
                    dve.scalar_tensor_tensor(out=out_t[:, m, :], in0=ps_y2, scalar=dn2[:, m:m + 1],
                                             in1=base2[:, m, :], op0=ALU.mult, op1=ALU.add).then_inc(s_out, 1)
                if live(c1, i):
                    wait(dve, s_t1h, i, c1)
                    wait(dve, s_y1[NCH - 1], i, c1 - 1)
                    dve.tensor_tensor(t1l[:, :], ps_t1[:, :], t1h[:, :].bitcast(F32), ALU.subtract)\
                       .then_inc(s_t1l, 1)
                    m = c1 % 2
                    wait(dve, s_dn1, i, c1)
                    wait(dve, s_out, i, c1 - 2)
                    wait(dve, s_base2, i, c1 - 2)
                    dve.tensor_scalar(dn2[:, m:m + 1], dn1[:, m:m + 1], DN2_SCALE / DN1_SCALE, None, ALU.mult)\
                       .then_inc(s_dn2, 1)
                if live(a, i):
                    m = a % 2
                    wait(dve, s_t0, i, a)
                    wait(dve, s_ln0, i, a)
                    wait(dve, s_base0, i, a - 1)
                    dve.tensor_scalar(s_in[:, :], ROW, rd0[:, m, 1:2], None, ALU.mult).then_inc(s_s, 1)
                    wait(dve, s_t0h, i, a)
                    wait(dve, s_y0, i, a - 1)
                    dve.tensor_tensor(t0l[:, :], ps_t0[:, :], t0h[:, :].bitcast(F32), ALU.subtract)\
                       .then_inc(s_t0l, 1)
                if live(c2, i):
                    wait(dve, s_t2h, i, c2)
                    wait(dve, s_y2, i, c2 - 1)
                    dve.tensor_tensor(t2l[:, :], ps_t2[:, :], t2h[:, :].bitcast(F32), ALU.subtract)\
                       .then_inc(s_t2l, 1)
                if live(p, i):
                    m = p % 2
                    wait_dma(dve, s_x, i, p)
                    dve.bn_stats(raw0[:, :], x_t[:, m, :]).then_inc(s_raw0, 1)
                    wait_dma(dve, s_adj, i, p, 32)
                    dve.scalar_tensor_tensor(out=hit[:, :], in0=adj_t[:, m, :], scalar=0.0, in1=wrow_t[:, m, :],
                                             op0=ALU.not_equal, op1=ALU.mult, accum_out=deg[:, m:m + 1])\
                       .then_inc(s_deg, 1)
                    wait(dve, s_ln0, i, p - 2)
                    wait(dve, s_raw0, i, p)
                    dve.reduce_sum(st0[:, m, 2:3], adj_t[:, m, :], AX.X)
                    dve.bn_aggr(st0[:, m, 0:2], raw0[:, :]).then_inc(s_stat0, 1)
                if live(c1, i):
                    m = c1 % 2
                    for c in range(NCH):
                        cols = slice(c * CH, (c + 1) * CH)
                        wait(dve, s_y1[c], i, c1)
                        wait(dve, s_h[c], i, c1 - 1)
                        dve.scalar_tensor_tensor(out=z[:, cols], in0=ps_y1[:, cols], scalar=dn1[:, m:m + 1],
                                                 in1=b1_all[:, cols], op0=ALU.mult, op1=ALU.add)\
                           .then_inc(s_z[c], 1)
                if live(p, i):
                    m = p % 2
                    wait(dve, s_at, i, p)
                    wait(dve, s_t0, i, p - 2)
                    dve.tensor_tensor(ahat_T[:, m, :], AT, ident[:, :], ALU.add).then_inc(s_ahat, 1)
                    wait(dve, s_p, i, p - 2)
                    dve.tensor_scalar(H_T[:, m, :], AT, 0.0, None, ALU.not_equal, ALU.add,
                                      accum_out=cnt[:, m:m + 1]).then_inc(s_cnt, 1)
                if live(a, i):
                    m = a % 2
                    wait(dve, s_deg, i, a)
                    dve.tensor_scalar(inv_d[:, :], deg[:, m:m + 1], TINY, 1.0 / DN1_SCALE, ALU.max, ALU.mult)\
                       .then_inc(s_degsafe, 1)
                if live(p, i):
                    m = p % 2
                    wait(dve, s_cnt, i, p)
                    dve.tensor_scalar(inv_b[:, :], cnt[:, m:m + 1], 1.0, 1.0 / P_SCALE, ALU.max, ALU.mult)\
                       .then_inc(s_cntsafe, 1)
                if live(a, i):
                    wait(dve, s_degsafe, i, a)
                    dve.reciprocal(inv_r[:, :], inv_d[:, :]).then_inc(s_deginv, 1)
                if live(p, i):
                    wait(dve, s_cntsafe, i, p)
                    dve.reciprocal(inv_t[:, :], inv_b[:, :]).then_inc(s_cntinv, 1)
                if live(a, i):
                    m = a % 2
                    wait(dve, s_deginv, i, a)
                    dve.scalar_tensor_tensor(out=dn1[:, m:m + 1], in0=deg[:, m:m + 1], scalar=0.0,
                                             in1=inv_r[:, :], op0=ALU.is_gt, op1=ALU.mult).then_inc(s_dn1, 1)
                if live(p, i):
                    m = p % 2
                    wait(dve, s_cntinv, i, p)
                    dve.tensor_scalar(HB_hi[:, m, :], H_T[:, m, :], inv_t[:, :], None, ALU.mult)\
                       .then_inc(s_hbhi, 1)
                if live(c1, i):
                    for c in range(NCH):
                        wait(dve, s_h[c], i, c1)
                        last = dve.bn_stats(raw2[:, c, :], h[:, c * CH:(c + 1) * CH])
                    last.then_inc(s_raw2, 1)
                if live(c1, i):
                    wait(dve, s_raw2, i, c1)
                    wait(dve, s_ln2, i, c1 - 1)
                if live(p, i):
                    m = p % 2
                    wait(dve, s_hbhi, i, p)
                    dve.scalar_tensor_tensor(out=HB_lo[:, m, :], in0=H_T[:, m, :], scalar=inv_t[:, :],
                                             in1=HB_hi[:, m, :], op0=ALU.mult, op1=ALU.subtract)\
                       .then_inc(s_ht, 1)
                if live(c1, i):
                    dve.bn_aggr(st2[:, :], raw2[:, :, :].rearrange("p c s -> p (c s)")).then_inc(s_stat2, 1)
                if live(a, i):
                    m = a % 2
                    wait(dve, s_y0, i, a)
                    wait(dve, s_base0, i, a)
                    wait(dve, s_base2, i, a - 2)
                    wait(dve, s_xh, i, a - 2)
                    dve.scalar_tensor_tensor(out=x1[:, m, :], in0=ps_y0[:, :], scalar=rd0[:, m, 1:2],
                                             in1=base0[:, :], op0=ALU.mult, op1=ALU.add).then_inc(s_x1, 1)
                    wait(dve, s_x1, i, a)
                    dve.bn_stats(raw1[:, :], x1[:, m, :]).then_inc(s_raw1, 1)
                    wait(dve, s_ph, i, a)
                    wait(dve, s_t2, i, a - 2)
                    wait(dve, s_raw1, i, a)
                    wait(dve, s_ln1, i, a - 1)
                    dve.tensor_tensor(P_lo[:, m, :], PP, P_hi[:, m, :], ALU.subtract).then_inc(s_pl, 1)
                    dve.bn_aggr(st1[:, :], raw1[:, :]).then_inc(s_stat1, 1)
                if isinstance(i, int) and c1 == 0:
                    tail_of_weights()
                if live(a, i):
                    m = a % 2
                    wait(dve, s_xhh, i, a)
                    wait(dve, s_t1, i, a - 1)
                    dve.scalar_tensor_tensor(out=xh_lo[:, :], in0=xh[:, m, :], scalar=X_SCALE, in1=xh_hi[:, :],
                                             op0=ALU.mult, op1=ALU.subtract).then_inc(s_xhl, 1)
                if live(c1, i):
                    wait(dve, s_hnh, i, c1)
                    wait(dve, s_t2, i, c1 - 1)
                    dve.scalar_tensor_tensor(out=hn_lo[:, :], in0=hn[:, :], scalar=H_SCALE, in1=hn_hi[:, :],
                                             op0=ALU.mult, op1=ALU.subtract).then_inc(s_hnl, 1)

            every_step(ENG.DVE, step)

        @block.gpsimd
        def _(pool):
            pool.memset(neg_half[:, :], -0.5)
            pool.memset(neg_one[:, :], -1.0)
            pool.memset(eps_one[:, 0:1], EPS)
            pool.memset(eps_one[:, 1:2], 1.0)
            pool.memset(ident[:, :], 0.0).then_inc(s_zero, 1)
            pool.wait_ge(s_zero, 1)
            pool.affine_select(out=ident[:, :], in_=ident[:, :], compare_op=ALU.not_equal, fill=1.0,
                               base=0, pattern=[[-1, 128]], channel_multiplier=1).then_inc(s_const, 1)
            pool.wait_ge(s_const, 1)

            def step(i, k):
                p, a, c1, o = k + 1, k, k - 1, k - 3
                if live(a, i):
                    m = a % 2
                    if isinstance(i, int) and a == 0:
                        pool.wait_ge(s_small, 5 * 16)
                    wait(pool, s_s, i, a)
                    wait(pool, s_base0, i, a - 1)
                    pool.tensor_tensor(scr0[:, :], b_all[:, :], s_in[:, :].to_broadcast([128, DIN]), ALU.mult).then_inc(s_pscr0, 1)
                    wait(pool, s_pscr0, i, a)
                    wait_dma(pool, s_x, i, a)
                    wait(pool, s_x1, i, a - 1)
                    pool.tensor_tensor(base0[:, :], scr0[:, :], x_t[:, m, :], ALU.add).then_inc(s_base0, 1)
                if live(p, i):
                    m = p % 2
                    wait(pool, s_stat0, i, p)
                    pool.tensor_tensor(pw0[:, :], st0[:, m, 1:3], eps_one[:, :], ALU.add).then_inc(s_pe0, 1)
                    wait(pool, s_pe0, i, p)
                    wait(pool, s_x1, i, p - 2)
                    wait(pool, s_h0, i, p - 2)
                    pool.tensor_tensor(nm0[:, :], st0[:, m, 0:1], neg_one[:, :], ALU.mult)
                    pool.tensor_tensor(rd0[:, m, :], pw0[:, :], neg_half[:, :], ALU.pow).then_inc(s_pp0, 1)
                    wait(pool, s_pp0, i, p)
                    pool.tensor_tensor(sc0[:, m, 0:1], rd0[:, m, 0:1], rd0[:, m, 1:2], ALU.mult)\
                        .then_inc(s_pr0, 1)
                    wait(pool, s_pr0, i, p)
                    pool.tensor_tensor(sc0[:, m, 1:2], nm0[:, :], sc0[:, m, 0:1], ALU.mult).then_inc(s_ln0, 1)
                if live(c1, i):
                    m = c1 % 2
                    wait(pool, s_x1, i, c1)
                    wait(pool, s_xh, i, c1)
                    wait(pool, s_base2, i, c1 - 1)
                    pool.tensor_tensor(scr2[:, :], x1[:, m, :], xh[:, m, :], ALU.add).then_inc(s_psum2a, 1)
                    wait(pool, s_psum2a, i, c1)
                    pool.tensor_tensor(sum2[:, :], scr2[:, :], b2_all[:, :], ALU.add).then_inc(s_psum2b, 1)
                    wait(pool, s_psum2b, i, c1)
                    wait(pool, s_dn2, i, c1)
                    wait(pool, s_ph, i, c1)
                    if isinstance(i, int) and c1 == 0:
                        pool.wait_ge(s_v, 1)
                    pool.tensor_tensor(q_dn[:, :], q[:, m:m + 1], dn2[:, m:m + 1], ALU.mult).then_inc(s_qdn, 1)
                    wait(pool, s_qdn, i, c1)
                    pool.tensor_tensor(scr2[:, :], v_all[:, :], q_dn[:, :].to_broadcast([128, DIN]), ALU.mult)\
                        .then_inc(s_psum2c, 1)
                    wait(pool, s_psum2c, i, c1)
                    wait(pool, s_out, i, c1 - 2)
                    pool.tensor_tensor(base2[:, m, :], sum2[:, :], scr2[:, :], ALU.add).then_inc(s_base2, 1)
                    wait(pool, s_stat2, i, c1)
                    pool.tensor_tensor(pw2[:, :], st2[:, 1:2], eps_one[:, 0:1], ALU.add).then_inc(s_pe2, 1)
                    pool.tensor_tensor(nm2[:, :], st2[:, 0:1], neg_one[:, :], ALU.mult)
                    wait(pool, s_pe2, i, c1)
                    wait(pool, s_hn, i, c1 - 1)
                    pool.tensor_tensor(sc2[:, 0:1], pw2[:, :], neg_half[:, 0:1], ALU.pow).then_inc(s_pp2, 1)
                    wait(pool, s_pp2, i, c1)
                    pool.tensor_tensor(sc2[:, 1:2], nm2[:, :], sc2[:, 0:1], ALU.mult).then_inc(s_ln2, 1)
                if live(a, i):
                    wait(pool, s_stat1, i, a)
                    pool.tensor_tensor(pw1[:, :], st1[:, 1:2], eps_one[:, 0:1], ALU.add).then_inc(s_pe1, 1)
                    pool.tensor_tensor(nm1[:, :], st1[:, 0:1], neg_one[:, :], ALU.mult)
                    wait(pool, s_pe1, i, a)
                    wait(pool, s_xh, i, a - 1)
                    pool.tensor_tensor(sc1[:, 0:1], pw1[:, :], neg_half[:, 0:1], ALU.pow).then_inc(s_pp1, 1)
                    wait(pool, s_pp1, i, a)
                    pool.tensor_tensor(sc1[:, 1:2], nm1[:, :], sc1[:, 0:1], ALU.mult).then_inc(s_ln1, 1)

            every_step(ENG.Pool, step)


def kernel(**inputs):
    import numpy as _np
    import concourse.bacc as _bacc
    from concourse import mybir as _mybir
    from concourse.bass_utils import run_bass_kernel_spmd as _run

    order = [
        ("x", inputs["x"]),
        ("adj", inputs["adj"]),
        ("W", inputs["L0_gnn_W"]),
        ("b", inputs["L0_gnn_b"]),
        ("W1T", _np.asarray(inputs["L1_gnn_W1"]).T),
        ("b1", inputs["L1_gnn_b1"]),
        ("gamma", _np.asarray(inputs["L1_gnn_gamma"]).reshape(-1, 128).T),
        ("beta", _np.asarray(inputs["L1_gnn_beta"]).reshape(-1, 128).T),
        ("W2T", _np.asarray(inputs["L1_gnn_W2"]).T),
        ("b2", inputs["L1_gnn_b2"]),
    ]
    nc = _bacc.Bacc("TRN2", target_bir_lowering=False, num_devices=1)
    arrays, args = {}, []
    for name, value in order:
        a = _np.ascontiguousarray(value)
        arrays[f"in_{name}_dram"] = a
        args.append(nc.dram_tensor(f"in_{name}_dram", a.shape, _mybir.dt.from_np(a.dtype), kind="ExternalInput").ap())
    shape = arrays["in_x_dram"].shape
    args.append(nc.dram_tensor("out_0_dram", shape, _mybir.dt.from_np(_np.dtype("float32")), kind="ExternalOutput").ap())
    bass_adjacency_prenorm_two_layer_gnn_kernel(nc, *args)
    r = _run(nc, [arrays], core_ids=[0])
    return r.results[0]["out_0_dram"]
```

```python
import concourse.bass as bass
from concourse import mybir
from contextlib import ExitStack


def bass_adjacency_prenorm_two_layer_gnn_kernel(
    nc: bass.Bass,
    x: bass.AP,
    adj: bass.AP,
    W: bass.AP,
    b: bass.AP,
    W1T: bass.AP,
    b1: bass.AP,
    gamma: bass.AP,
    beta: bass.AP,
    W2T: bass.AP,
    b2: bass.AP,
    out: bass.AP,
):
    F32, F32R, F16 = mybir.dt.float32, mybir.dt.float32r, mybir.dt.float16
    ALU = mybir.AluOpType
    ACT = mybir.ActivationFunctionType
    AX = mybir.AxisListType
    ENG = mybir.EngineType

    NG, N, DIN = x.shape
    DH = W1T.shape[1]
    CH = 512
    KI, KH = DIN // 128, DH // 128
    NCH = DH // CH
    EPS = 1e-5
    P_SCALE = 2.0 ** 8
    X_SCALE = 2.0 ** 11
    H_SCALE = 2.0 ** 10
    DN1_SCALE = 1.0 / (P_SCALE * X_SCALE)
    DN2_SCALE = 1.0 / (P_SCALE * H_SCALE)
    TINY = 1.1754944e-38
    SMALL = 5 * 16

    LOOP_FROM = 5
    LOOP_TO = NG - 1
    assert (LOOP_TO - LOOP_FROM) % 2 == 0 and LOOP_TO > LOOP_FROM
    ORDER = list(range(-1, LOOP_FROM)), list(range(LOOP_TO, NG + 3))

    ctx = ExitStack()
    with ctx:
        def sb(name, shape, dt=F32):
            return ctx.enter_context(nc.sbuf_tensor(name, shape, dt))

        def sem(name):
            return ctx.enter_context(nc.semaphore(name))

        stage = sb("stage", [128, 2, 4096])
        w0h, w0l = sb("w0h", [128, KI, DIN], F32R), sb("w0l", [128, KI, DIN], F32R)
        w1h, w1l = sb("w1h", [128, KI, DH], F32R), sb("w1l", [128, KI, DH], F32R)
        w2h, w2l = sb("w2h", [128, KH, DIN], F32R), sb("w2l", [128, KH, DIN], F32R)
        gam, bet = sb("gam", [128, KH]), sb("bet", [128, KH])
        bet_wide = sb("bet_wide", [128, KH, 128])
        b_all, b1_all, b2_all = sb("b_all", [128, DIN]), sb("b1_all", [128, DH]), sb("b2_all", [128, DIN])
        v_all = sb("v_all", [128, DIN])
        ident = sb("ident", [128, 128])
        neg_half = sb("neg_half", [128, 2])
        neg_one = sb("neg_one", [128, 1])
        h_scale = sb("h_scale", [128, 1])
        eps_one = sb("eps_one", [128, 2])

        raw_w0 = stage[:, 0, 0:KI * DIN].rearrange("p (t n) -> p t n", t=KI)
        raw_w1 = stage[:, 1, :].rearrange("p (t n) -> p t n", t=KI)
        raw_w2 = stage[:, 0, :].rearrange("p (t n) -> p t n", t=KH)

        x_t = sb("x_t", [128, 2, DIN])
        adj_t = sb("adj_t", [128, 2, N])
        wrow_t = sb("wrow_t", [128, 2, N])
        hit = sb("hit", [128, N])
        ahat_T = sb("ahat_T", [128, 2, N])
        H_T = sb("H_T", [128, 2, N], F16)
        HB_hi, HB_lo = sb("HB_hi", [128, 2, N], F16), sb("HB_lo", [128, 2, N], F16)
        P_hi, P_lo = sb("P_hi", [128, 2, N], F16), sb("P_lo", [128, 2, N], F16)
        h0 = sb("h0", [128, 2, DIN])
        t0h, t0l = sb("t0h", [128, DIN], F32R), sb("t0l", [128, DIN], F32R)
        t1h, t1l = sb("t1h", [128, DIN], F32R), sb("t1l", [128, DIN], F32R)
        t2h, t2l = sb("t2h", [128, DH], F32R), sb("t2l", [128, DH], F32R)
        base0, scr0 = sb("base0", [128, DIN]), sb("scr0", [128, DIN])
        x1 = sb("x1", [128, 2, DIN])
        xh = sb("xh", [128, 2, DIN])
        xh_hi, xh_lo = sb("xh_hi", [128, DIN], F16), sb("xh_lo", [128, DIN], F16)
        z, h = sb("z", [128, DH]), sb("h", [128, DH])
        hn = sb("hn", [128, DH])
        hn_hi, hn_lo = sb("hn_hi", [128, DH], F16), sb("hn_lo", [128, DH], F16)
        sum2, scr2 = sb("sum2", [128, DIN]), sb("scr2", [128, DIN])
        vq = sb("vq", [128, DIN])
        base2 = sb("base2", [128, 2, DIN])
        out_t = sb("out_t", [128, 2, DIN])
        raw0, raw1, raw2 = sb("raw0", [128, 6]), sb("raw1", [128, 6]), sb("raw2", [128, NCH, 6])
        st0 = sb("st0", [128, 2, 3])
        st1, st2 = sb("st1", [128, 2]), sb("st2", [128, 2])
        pw0, pw1, pw2 = sb("pw0", [128, 2]), sb("pw1", [128, 1]), sb("pw2", [128, 1])
        pz2 = sb("pz2", [128, 1])
        rd0 = sb("rd0", [128, 2, 2])
        sc0, sc1, sc2 = sb("sc0", [128, 2, 2]), sb("sc1", [128, 2]), sb("sc2", [128, 2])
        nm0, nm1, nm2 = sb("nm0", [128, 1]), sb("nm1", [128, 1]), sb("nm2", [128, 1])
        qdn = sb("qdn", [128, 1])
        s_in = sb("s_in", [128, 1])
        deg, cnt = sb("deg", [128, 2]), sb("cnt", [128, 2])
        inv_b, inv_t = sb("inv_b", [128, 1]), sb("inv_t", [128, 1])
        inv_d, inv_r = sb("inv_d", [128, 1]), sb("inv_r", [128, 1])
        dn1, dn2 = sb("dn1", [128, 2]), sb("dn2", [128, 2])
        q = sb("q", [128, 2])

        def bank(name, n=1):
            return ctx.enter_context(nc.psum_tensor(name, [128, n * CH], F32))

        ps_t2 = bank("ps_t2", 2)
        ps_y1 = bank("ps_y1", 2)
        ps_t1 = bank("ps_t1")
        ps_t0 = bank("ps_t0")
        ps_at = bank("ps_at")
        ps_p = bank("ps_p")
        ps_y0 = ps_t1
        ps_y2 = ps_t2[:, 0:CH]
        AT = ps_at[:, 0:N]
        ROW = ps_at[:, N:N + 1]
        PP = ps_p[:, 0:N]

        s_const = sem("consts_built")
        s_small = sem("small_params_loaded")
        s_stage = [sem("stage_loaded_0"), sem("stage_loaded_1")]
        s_whi = sem("weights_hi_split")
        s_wlo = sem("weights_lo_split")
        s_betw = sem("beta_widened")
        s_vps = sem("v_in_psum")
        s_v = sem("v_ready")
        s_x = [sem("x_loaded_0"), sem("x_loaded_1")]
        s_adj = [sem("adj_loaded_0"), sem("adj_loaded_1")]
        s_st = [sem("out_stored_0"), sem("out_stored_1")]
        s_zero = sem("ident_zeroed")
        s_at, s_ahat, s_ht = sem("adjT_in_psum"), sem("ahatT_ready"), sem("HT_parts_ready")
        s_stat0, s_ln0, s_h0 = sem("stats0_ready"), sem("ln0_scalars_ready"), sem("h0_ready")
        s_t0, s_t0h, s_t0l = sem("t0_in_psum"), sem("t0_hi_ready"), sem("t0_lo_ready")
        s_s, s_scr0, s_base0 = sem("bias0_factor_ready"), sem("bias0_rows_ready"), sem("base0_ready")
        s_qdn, s_vq = sem("q_dn_product"), sem("beta_rows_ready")
        s_y0, s_x1 = sem("y0_in_psum"), sem("x1_ready")
        s_stat1, s_ln1, s_xh = sem("stats1_ready"), sem("ln1_scalars_ready"), sem("xh_ready")
        s_xhh, s_xhl = sem("xh_hi_ready"), sem("xh_lo_ready")
        s_p, s_ph, s_pl = sem("P_in_psum"), sem("P_hi_ready"), sem("P_lo_ready")
        s_t1, s_t1h, s_t1l = sem("t1_in_psum"), sem("t1_hi_ready"), sem("t1_lo_ready")
        s_y1 = [sem(f"y1_chunk{c}_in_psum") for c in range(NCH)]
        s_z = [sem(f"z_chunk{c}_ready") for c in range(NCH)]
        s_h = [sem(f"h_chunk{c}_ready") for c in range(NCH)]
        s_stat2, s_ln2, s_hn = sem("stats2_ready"), sem("ln2_scalars_ready"), sem("hn_ready")
        s_hnh, s_hnl = sem("hn_hi_ready"), sem("hn_lo_ready")
        s_dn2, s_base2 = sem("dn2_ready"), sem("base2_ready")
        s_t2, s_t2h, s_t2l = sem("t2_in_psum"), sem("t2_hi_ready"), sem("t2_lo_ready")
        s_y2, s_out = sem("y2_in_psum"), sem("out_ready")
        s_raw0, s_raw1, s_raw2 = sem("bn_raw0_ready"), sem("bn_raw1_ready"), sem("bn_raw2_ready")
        s_deg, s_degsafe, s_deginv, s_dn1 = sem("deg_ready"), sem("deg_safe"), sem("deg_inverted"), sem("dn1_ready")
        s_cnt, s_cntsafe, s_cntinv, s_hbhi = sem("cnt_ready"), sem("cnt_safe"), sem("cnt_inverted"), sem("HB_hi_ready")
        s_pe0, s_pp0, s_pr0 = sem("ln0_var_eps"), sem("ln0_rstd_and_D"), sem("ln0_rstd_D_product")
        s_pe1, s_pp1 = sem("ln1_var_eps"), sem("ln1_rstd")
        s_pe2, s_pz2, s_pp2 = sem("ln2_var_eps"), sem("ln2_var_scaled"), sem("ln2_rstd")
        s_psum2a, s_psum2b = sem("x1_plus_xh"), sem("x1_xh_b2_sum")

        def live(g, i):
            return not isinstance(i, int) or 0 <= g < NG

        def wait(eng, s, i, g):
            if not isinstance(i, int) or g >= 0:
                eng.wait_ge(s, i + (g + 1))

        def wait_chunks(eng, s, i, g):
            eng.wait_ge(s, i * NCH + NCH * (g + 1))

        def wait_dma(eng, pair, i, g, each=16):
            if not isinstance(i, int) or g >= 0:
                eng.wait_ge(pair[g % 2], i * (each // 2) + each * (g // 2 + 1))

        def every_step(eng_type, step):
            for k in ORDER[0]:
                step(0, k)
            with nc.Fori(0, LOOP_TO - LOOP_FROM, 2, engines=(eng_type,), hint_back_edge=True) as i:
                step(i, LOOP_FROM)
                step(i, LOOP_FROM + 1)
            for k in ORDER[1]:
                step(0, k)

        block = ctx.enter_context(nc.Block())

        @block.sync
        def _(sp):
            def load_adj(i, g):
                n = g % 2
                at = bass.ds(i + g, 1)
                sp.dma_start(adj_t[:, n, :], adj[at, :, :].rearrange("g n e -> n (g e)")).then_inc(s_adj[n], 16)
                sp.dma_start(wrow_t[:, n, :], adj[at, 0, :].to_broadcast([128, N])).then_inc(s_adj[n], 16)

            def load_x(i, g):
                sp.dma_start(x_t[:, g % 2, :], x[bass.ds(i + g, 1), :, :].rearrange("g n f -> n (g f)"))\
                  .then_inc(s_x[g % 2], 16)

            load_adj(0, 0)
            load_x(0, 0)
            sp.dma_start(raw_w0, W.rearrange("(t p) n -> p t n", p=128)).then_inc(s_stage[0], 16)
            sp.dma_start(raw_w1, W1T.rearrange("(t p) n -> p t n", p=128)).then_inc(s_stage[1], 16)
            for row, src in ((b_all, b), (b1_all, b1), (b2_all, b2)):
                sp.dma_start(row[:, :], src.rearrange("(a n) -> a n", a=1).to_broadcast([128, src.shape[0]]))\
                  .then_inc(s_small, 16)
            for col, src in ((gam, gamma), (bet, beta)):
                sp.dma_start(col[:, :], src).then_inc(s_small, 16)
            load_adj(0, 1)
            load_x(0, 1)
            sp.wait_ge(s_whi, 1)
            sp.wait_ge(s_wlo, 1)
            sp.dma_start(raw_w2, W2T.rearrange("(t p) n -> p t n", p=128)).then_inc(s_stage[0], 16)

            def step(i, k):
                g, o = k + 2, k - 3
                if live(o, i):
                    wait(sp, s_out, i, o)
                    sp.dma_start(out[bass.ds(i + o, 1), :, :].rearrange("g n f -> n (g f)"), out_t[:, o % 2, :])\
                      .then_inc(s_st[o % 2], 16)
                if isinstance(i, int) and not 2 <= g < NG:
                    return
                wait(sp, s_stat0, i, g - 2)
                wait(sp, s_at, i, g - 2)
                load_adj(i, g)
                wait(sp, s_h0, i, g - 2)
                wait(sp, s_base0, i, g - 2)
                load_x(i, g)

            for k in ORDER[0]:
                step(0, k)
            with nc.Fori(0, LOOP_TO - LOOP_FROM - 2, 2, engines=(ENG.SP,), hint_back_edge=True) as i:
                step(i, LOOP_FROM)
                step(i, LOOP_FROM + 1)
            for k in [LOOP_TO - 2, LOOP_TO - 1] + ORDER[1]:
                step(0, k)
            for g in (NG - 2, NG - 1):
                wait_dma(sp, s_st, 0, g)

        @block.tensor
        def _(pe):
            def thin(ps, lhs, rhs):
                (lh, ll), (rh, rl) = lhs, rhs
                pe.matmul(ps, lh, rh, start=True, stop=False)
                pe.matmul(ps, lh, rl, start=False, stop=False)
                return pe.matmul(ps, ll, rh, start=False, stop=True)

            def incidence_product(i, g):
                m = g % 2
                wait(pe, s_ht, i, g)
                wait(pe, s_pl, i, g - 1)
                pe.matmul(PP, HB_hi[:, m, :], H_T[:, m, :], start=True, stop=False)
                pe.matmul(PP, HB_lo[:, m, :], H_T[:, m, :], start=False, stop=True).then_inc(s_p, 1)

            def with_weights(ps, t_hi, t_lo, w_hi, w_lo, blocks, cols, low_ready, between=None):
                for n, (t, w) in enumerate(((t_hi, w_hi), (t_hi, w_lo), (t_lo, w_hi))):
                    if n == 2:
                        low_ready()
                    for j in range(blocks):
                        mm = pe.matmul(ps, t[:, j * 128:(j + 1) * 128], w[:, j, cols],
                                       start=(n == 0 and j == 0), stop=(n == 2 and j == blocks - 1))
                    if n == 0 and between is not None:
                        between()
                return mm

            def beta_row():
                pe.wait_ge(s_betw, 1)
                pe.wait_ge(s_stage[0], 32)
                for j in range(KH):
                    mm = pe.matmul(ps_y2, bet_wide[:, j, :], raw_w2[:, j, :], start=(j == 0), stop=(j == KH - 1))
                mm.then_inc(s_vps, 1)

            def step(i, k):
                p, a, c1, c2, o = k + 1, k, k - 1, k - 2, k - 3
                if isinstance(i, int) and c1 == 0:
                    beta_row()
                if live(a, i):
                    m = a % 2
                    wait(pe, s_ln0, i, a)
                    wait(pe, s_ahat, i, a)
                    wait(pe, s_cnt, i, a)
                    wait(pe, s_h0, i, a)
                    wait(pe, s_t0l, i, a - 1)
                    pe.matmul(ROW, ahat_T[:, m, :], rd0[:, m, 1:2], start=True, stop=True)
                    for j in range(KI):
                        f = slice(j * 128, (j + 1) * 128)
                        mm = pe.matmul(ps_t0[:, f], h0[:, m, f], ahat_T[:, m, :], start=True, stop=True)
                    mm.then_inc(s_t0, 1)
                if live(c1, i):
                    m = c1 % 2
                    wait(pe, s_xhh, i, c1)
                    wait(pe, s_xhl, i, c1)
                    wait(pe, s_pl, i, c1)
                    wait(pe, s_x1, i, c1)
                    for j in range(KI):
                        f = slice(j * 128, (j + 1) * 128)
                        mm = thin(ps_t1[:, f], (xh_hi[:, f], xh_lo[:, f]), (P_hi[:, m, :], P_lo[:, m, :]))
                    mm.then_inc(s_t1, 1)
                if live(c2, i):
                    m = c2 % 2
                    wait(pe, s_hnh, i, c2)
                    wait(pe, s_hnl, i, c2)
                    wait(pe, s_t2l, i, c2 - 1)
                    if isinstance(i, int) and c2 == 0:
                        pe.wait_ge(s_v, 1)
                    for j in [*range(KH // 2, KH), *range(KH // 2)]:
                        if j == 0:
                            wait(pe, s_out, i, o)
                        f = slice(j * 128, (j + 1) * 128)
                        mm = thin(ps_t2[:, f], (hn_hi[:, f], hn_lo[:, f]), (P_hi[:, m, :], P_lo[:, m, :]))
                    mm.then_inc(s_t2, 1)
                if live(c1, i):
                    if isinstance(i, int) and c1 == 0:
                        pe.wait_ge(s_wlo, 2)
                        pe.wait_ge(s_whi, 2)
                    wait(pe, s_t1h, i, c1)
                    for c in range(NCH):
                        wait(pe, s_z[c], i, c1 - 1)
                        cols = slice(c * CH, (c + 1) * CH)
                        with_weights(ps_y1[:, cols], t1h, t1l, w1h, w1l, KI, cols,
                                     low_ready=lambda: wait(pe, s_t1l, i, c1)).then_inc(s_y1[c], 1)
                if live(p, i):
                    wait_dma(pe, s_adj, i, p, 32)
                    if isinstance(i, int) and p == 0:
                        pe.wait_ge(s_const, 1)
                    wait(pe, s_s, i, a)
                    pe.transpose(AT, adj_t[:, p % 2, :], ident[:, :]).then_inc(s_at, 1)
                if live(a, i):
                    if isinstance(i, int) and a == 0:
                        pe.wait_ge(s_wlo, 1)
                        pe.wait_ge(s_whi, 1)
                    wait(pe, s_t1l, i, c1)
                    wait(pe, s_t0h, i, a)
                    with_weights(ps_y0[:, :], t0h, t0l, w0h, w0l, KI, slice(0, DIN),
                                 low_ready=lambda: wait(pe, s_t0l, i, a)).then_inc(s_y0, 1)
                if live(a, i) and not live(c2, i):
                    incidence_product(i, a)
                if live(c2, i):
                    if isinstance(i, int) and c2 == 0:
                        pe.wait_ge(s_wlo, 3)
                        pe.wait_ge(s_whi, 3)
                    wait(pe, s_t2h, i, c2)
                    wait(pe, s_t2l, i, c2)
                    with_weights(ps_y2, t2h, t2l, w2h, w2l, KH, slice(0, DIN), low_ready=lambda: None,
                                 between=(lambda: incidence_product(i, a)) if live(a, i) else None)\
                        .then_inc(s_y2, 1)

            every_step(ENG.PE, step)

        @block.scalar
        def _(act):
            def split_w0():
                act.wait_ge(s_stage[0], 16)
                act.activation(w0h[:, :, :], raw_w0, ACT.Copy).then_inc(s_whi, 1)

            def split_w1():
                act.wait_ge(s_stage[1], 16)
                act.activation(w1h[:, :, :], raw_w1, ACT.Copy).then_inc(s_whi, 1)

            def split_w2():
                act.wait_ge(s_stage[0], 32)
                act.wait_ge(s_small, SMALL)
                for j in range(KH):
                    last = act.activation(w2h[:, j, :], raw_w2[:, j, :], ACT.Copy, scale=gam[:, j:j + 1])
                last.then_inc(s_whi, 1)

            def relu_chunk(i, g, c):
                cols = slice(c * CH, (c + 1) * CH)
                wait(act, s_z[c], i, g)
                act.activation(h[:, cols], z[:, cols], ACT.Relu).then_inc(s_h[c], 1)

            def step(i, k):
                p, a, c1, c2 = k + 1, k, k - 1, k - 2
                if isinstance(i, int) and a == 0:
                    split_w0()
                if live(c1, i):
                    wait(act, s_t1, i, c1)
                    wait(act, s_y1[NCH - 1], i, c1 - 1)
                    act.activation(t1h[:, :], ps_t1[:, :], ACT.Copy).then_inc(s_t1h, 1)
                if live(a, i):
                    wait(act, s_t0, i, a)
                    wait(act, s_y0, i, a - 1)
                    act.activation(t0h[:, :], ps_t0[:, :], ACT.Copy).then_inc(s_t0h, 1)
                if live(c2, i):
                    wait(act, s_t2, i, c2)
                    wait(act, s_y2, i, c2 - 1)
                    act.activation(t2h[:, :], ps_t2[:, :], ACT.Copy).then_inc(s_t2h, 1)
                if live(a, i):
                    wait(act, s_s, i, a)
                    if isinstance(i, int) and a == 0:
                        act.wait_ge(s_small, SMALL)
                    wait(act, s_base0, i, a - 1)
                    act.activation(scr0[:, :], b_all[:, :], ACT.Copy, scale=s_in[:, :]).then_inc(s_scr0, 1)
                if isinstance(i, int) and a == 0:
                    split_w1()
                if live(c1, i):
                    wait(act, s_qdn, i, c1)
                    if isinstance(i, int) and c1 == 0:
                        act.wait_ge(s_v, 1)
                    wait(act, s_base2, i, c1 - 1)
                    act.activation(vq[:, :], v_all[:, :], ACT.Copy, scale=qdn[:, :]).then_inc(s_vq, 1)
                    wait(act, s_stat2, i, c1 - 1)
                    wait(act, s_hn, i, c1 - 1)
                    wait(act, s_hnh, i, c1 - 1)
                    relu_chunk(i, c1, 0)
                if live(p, i):
                    m = p % 2
                    wait(act, s_ln0, i, p)
                    wait_dma(act, s_x, i, p)
                    wait(act, s_t0, i, p - 2)
                    act.activation(h0[:, m, :], x_t[:, m, :], ACT.Relu, bias=sc0[:, m, 1:2],
                                   scale=sc0[:, m, 0:1]).then_inc(s_h0, 1)
                if live(c1, i):
                    for c in range(1, NCH):
                        relu_chunk(i, c1, c)
                    wait(act, s_ln2, i, c1)
                    wait(act, s_h[NCH - 1], i, c1)
                    wait(act, s_t2, i, c1 - 1)
                    act.activation(hn_hi[:, :], h[:, :], ACT.Identity, bias=sc2[:, 1:2],
                                   scale=sc2[:, 0:1]).then_inc(s_hnh, 1)
                if live(a, i):
                    m = a % 2
                    wait(act, s_p, i, a)
                    wait(act, s_t2, i, a - 2)
                    wait(act, s_base2, i, a - 2)
                    act.activation(P_hi[:, m, :], PP, ACT.Copy, accum_out=q[:, m:m + 1]).then_inc(s_ph, 1)
                if live(a, i):
                    m = a % 2
                    wait(act, s_ln1, i, a)
                    wait(act, s_base2, i, a - 2)
                    wait(act, s_xhl, i, a - 2)
                    act.activation(xh[:, m, :], x1[:, m, :], ACT.Relu, bias=sc1[:, 1:2],
                                   scale=sc1[:, 0:1]).then_inc(s_xh, 1)
                    wait(act, s_xh, i, a)
                    wait(act, s_t1, i, a - 1)
                    act.activation(xh_hi[:, :], xh[:, m, :], ACT.Copy, scale=X_SCALE).then_inc(s_xhh, 1)
                if isinstance(i, int) and c1 == 0:
                    split_w2()

            every_step(ENG.Activation, step)

        @block.vector
        def _(dve):
            def split_w0():
                dve.wait_ge(s_whi, 1)
                dve.tensor_tensor(w0l[:, :, :], raw_w0, w0h[:, :, :].bitcast(F32), ALU.subtract).then_inc(s_wlo, 1)

            def split_w1():
                dve.wait_ge(s_whi, 2)
                dve.tensor_tensor(w1l[:, :, :], raw_w1, w1h[:, :, :].bitcast(F32), ALU.subtract).then_inc(s_wlo, 1)

            def widen_beta():
                dve.wait_ge(s_small, SMALL)
                dve.tensor_copy(bet_wide[:, :, :], bet[:, :].unsqueeze(2).to_broadcast([128, KH, 128]))\
                   .then_inc(s_betw, 1)

            def split_w2():
                dve.wait_ge(s_whi, 3)
                for j in range(KH):
                    last = dve.scalar_tensor_tensor(out=w2l[:, j, :], in0=raw_w2[:, j, :], scalar=gam[:, j:j + 1],
                                                    in1=w2h[:, j, :].bitcast(F32), op0=ALU.mult, op1=ALU.subtract)
                last.then_inc(s_wlo, 1)

            def scale_v():
                dve.wait_ge(s_vps, 1)
                dve.tensor_scalar(v_all[:, :], ps_y2, H_SCALE, None, ALU.mult).then_inc(s_v, 1)

            def stat2_chunk(i, g, c):
                wait(dve, s_h[c], i, g)
                dve.bn_stats(raw2[:, c, :], h[:, c * CH:(c + 1) * CH]).then_inc(s_raw2, 1)

            def step(i, k):
                p, a, c1, c2, o = k + 1, k, k - 1, k - 2, k - 3
                if live(o, i):
                    m = o % 2
                    wait(dve, s_y2, i, o)
                    wait(dve, s_base2, i, o)
                    wait(dve, s_dn2, i, o)
                    wait_dma(dve, s_st, i, o - 2)
                    dve.scalar_tensor_tensor(out=out_t[:, m, :], in0=ps_y2, scalar=dn2[:, m:m + 1],
                                             in1=base2[:, m, :], op0=ALU.mult, op1=ALU.add).then_inc(s_out, 1)
                if live(c1, i):
                    wait(dve, s_t1h, i, c1)
                    wait(dve, s_y1[NCH - 1], i, c1 - 1)
                    dve.tensor_tensor(t1l[:, :], ps_t1[:, :], t1h[:, :].bitcast(F32), ALU.subtract)\
                       .then_inc(s_t1l, 1)
                    m = c1 % 2
                    if isinstance(i, int) and c1 == 0:
                        scale_v()
                    wait(dve, s_dn1, i, c1)
                    wait(dve, s_out, i, c1 - 2)
                    dve.tensor_scalar(dn2[:, m:m + 1], dn1[:, m:m + 1], DN2_SCALE / DN1_SCALE, None, ALU.mult)\
                       .then_inc(s_dn2, 1)
                    wait(dve, s_vq, i, c1 - 1)
                    wait(dve, s_ph, i, c1)
                    dve.scalar_tensor_tensor(out=qdn[:, :], in0=dn1[:, m:m + 1], scalar=DN2_SCALE / DN1_SCALE,
                                             in1=q[:, m:m + 1], op0=ALU.mult, op1=ALU.mult).then_inc(s_qdn, 1)
                if live(a, i):
                    m = a % 2
                    wait(dve, s_t0, i, a)
                    wait(dve, s_ln0, i, a)
                    wait(dve, s_scr0, i, a - 1)
                    dve.tensor_scalar(s_in[:, :], ROW, rd0[:, m, 1:2], None, ALU.mult).then_inc(s_s, 1)
                    wait(dve, s_t0h, i, a)
                    wait(dve, s_y0, i, a - 1)
                    dve.tensor_tensor(t0l[:, :], ps_t0[:, :], t0h[:, :].bitcast(F32), ALU.subtract)\
                       .then_inc(s_t0l, 1)
                if isinstance(i, int) and a == 0:
                    split_w0()
                if live(c2, i):
                    wait(dve, s_t2h, i, c2)
                    wait(dve, s_y2, i, c2 - 1)
                    dve.tensor_tensor(t2l[:, :], ps_t2[:, :], t2h[:, :].bitcast(F32), ALU.subtract)\
                       .then_inc(s_t2l, 1)
                if live(p, i):
                    m = p % 2
                    wait_dma(dve, s_x, i, p)
                    dve.bn_stats(raw0[:, :], x_t[:, m, :]).then_inc(s_raw0, 1)
                    wait_dma(dve, s_adj, i, p, 32)
                    dve.scalar_tensor_tensor(out=hit[:, :], in0=adj_t[:, m, :], scalar=0.0, in1=wrow_t[:, m, :],
                                             op0=ALU.not_equal, op1=ALU.mult, accum_out=deg[:, m:m + 1])\
                       .then_inc(s_deg, 1)
                    wait(dve, s_ln0, i, p - 2)
                    wait(dve, s_raw0, i, p)
                    dve.reduce_sum(st0[:, m, 2:3], adj_t[:, m, :], AX.X)
                    dve.bn_aggr(st0[:, m, 0:2], raw0[:, :]).then_inc(s_stat0, 1)
                if live(c1, i):
                    m = c1 % 2
                    for c in range(NCH):
                        cols = slice(c * CH, (c + 1) * CH)
                        wait(dve, s_y1[c], i, c1)
                        wait(dve, s_h[c], i, c1 - 1)
                        dve.scalar_tensor_tensor(out=z[:, cols], in0=ps_y1[:, cols], scalar=dn1[:, m:m + 1],
                                                 in1=b1_all[:, cols], op0=ALU.mult, op1=ALU.add)\
                           .then_inc(s_z[c], 1)
                        if c < NCH - 1:
                            stat2_chunk(i, c1, c)
                if isinstance(i, int) and a == 0:
                    split_w1()
                    widen_beta()
                if live(p, i):
                    m = p % 2
                    wait(dve, s_at, i, p)
                    wait(dve, s_t0, i, p - 2)
                    dve.tensor_tensor(ahat_T[:, m, :], AT, ident[:, :], ALU.add).then_inc(s_ahat, 1)
                    wait(dve, s_p, i, p - 2)
                    dve.tensor_scalar(H_T[:, m, :], AT, 0.0, None, ALU.not_equal, ALU.add,
                                      accum_out=cnt[:, m:m + 1]).then_inc(s_cnt, 1)
                if live(p, i):
                    m = p % 2
                    wait(dve, s_cnt, i, p)
                    dve.tensor_scalar(inv_b[:, :], cnt[:, m:m + 1], 1.0, 1.0 / P_SCALE, ALU.max, ALU.mult)\
                       .then_inc(s_cntsafe, 1)
                if live(p, i):
                    wait(dve, s_cntsafe, i, p)
                    dve.reciprocal(inv_t[:, :], inv_b[:, :]).then_inc(s_cntinv, 1)
                if live(p, i):
                    m = p % 2
                    wait(dve, s_cntinv, i, p)
                    dve.tensor_scalar(HB_hi[:, m, :], H_T[:, m, :], inv_t[:, :], None, ALU.mult)\
                       .then_inc(s_hbhi, 1)
                if live(c1, i):
                    stat2_chunk(i, c1, NCH - 1)
                    wait_chunks(dve, s_raw2, i, c1)
                    wait(dve, s_ln2, i, c1 - 1)
                if live(p, i):
                    m = p % 2
                    wait(dve, s_hbhi, i, p)
                    dve.scalar_tensor_tensor(out=HB_lo[:, m, :], in0=H_T[:, m, :], scalar=inv_t[:, :],
                                             in1=HB_hi[:, m, :], op0=ALU.mult, op1=ALU.subtract)\
                       .then_inc(s_ht, 1)
                if live(c1, i):
                    dve.bn_aggr(st2[:, :], raw2[:, :, :].rearrange("p c s -> p (c s)")).then_inc(s_stat2, 1)
                if live(a, i):
                    m = a % 2
                    wait(dve, s_y0, i, a)
                    wait(dve, s_base0, i, a)
                    wait(dve, s_base2, i, a - 2)
                    wait(dve, s_xh, i, a - 2)
                    dve.scalar_tensor_tensor(out=x1[:, m, :], in0=ps_y0[:, :], scalar=rd0[:, m, 1:2],
                                             in1=base0[:, :], op0=ALU.mult, op1=ALU.add).then_inc(s_x1, 1)
                    wait(dve, s_x1, i, a)
                    dve.bn_stats(raw1[:, :], x1[:, m, :]).then_inc(s_raw1, 1)
                    wait(dve, s_raw1, i, a)
                    wait(dve, s_ln1, i, a - 1)
                    wait(dve, s_deg, i, a)
                    dve.tensor_scalar(inv_d[:, :], deg[:, m:m + 1], TINY, 1.0 / DN1_SCALE, ALU.max, ALU.mult)\
                       .then_inc(s_degsafe, 1)
                    dve.bn_aggr(st1[:, :], raw1[:, :]).then_inc(s_stat1, 1)
                if live(c1, i):
                    wait(dve, s_ln2, i, c1)
                    wait(dve, s_hnl, i, c1 - 1)
                    dve.tensor_scalar(hn[:, :], h[:, :], sc2[:, 0:1], sc2[:, 1:2], ALU.mult, ALU.add)\
                       .then_inc(s_hn, 1)
                if live(a, i):
                    m = a % 2
                    wait(dve, s_degsafe, i, a)
                    dve.reciprocal(inv_r[:, :], inv_d[:, :]).then_inc(s_deginv, 1)
                    wait(dve, s_deginv, i, a)
                    dve.scalar_tensor_tensor(out=dn1[:, m:m + 1], in0=deg[:, m:m + 1], scalar=0.0,
                                             in1=inv_r[:, :], op0=ALU.is_gt, op1=ALU.mult).then_inc(s_dn1, 1)
                    wait(dve, s_ph, i, a)
                    wait(dve, s_t2, i, a - 2)
                    dve.tensor_tensor(P_lo[:, m, :], PP, P_hi[:, m, :], ALU.subtract).then_inc(s_pl, 1)
                if live(c1, i):
                    wait(dve, s_hnh, i, c1)
                    wait(dve, s_hn, i, c1)
                    wait(dve, s_t2, i, c1 - 1)
                    dve.tensor_tensor(hn_lo[:, :], hn[:, :], hn_hi[:, :], ALU.subtract).then_inc(s_hnl, 1)
                if live(a, i):
                    m = a % 2
                    wait(dve, s_xhh, i, a)
                    wait(dve, s_t1, i, a - 1)
                    dve.scalar_tensor_tensor(out=xh_lo[:, :], in0=xh[:, m, :], scalar=X_SCALE, in1=xh_hi[:, :],
                                             op0=ALU.mult, op1=ALU.subtract).then_inc(s_xhl, 1)
                if isinstance(i, int) and c1 == 0:
                    split_w2()

            every_step(ENG.DVE, step)

        @block.gpsimd
        def _(pool):
            pool.memset(neg_half[:, :], -0.5)
            pool.memset(neg_one[:, :], -1.0)
            pool.memset(h_scale[:, :], H_SCALE ** -2)
            pool.memset(eps_one[:, 0:1], EPS)
            pool.memset(eps_one[:, 1:2], 1.0)
            pool.memset(ident[:, :], 0.0).then_inc(s_zero, 1)
            pool.wait_ge(s_zero, 1)
            pool.affine_select(out=ident[:, :], in_=ident[:, :], compare_op=ALU.not_equal, fill=1.0,
                               base=0, pattern=[[-1, 128]], channel_multiplier=1).then_inc(s_const, 1)
            pool.wait_ge(s_const, 1)

            def step(i, k):
                p, a, c1, o = k + 1, k, k - 1, k - 3
                if live(a, i):
                    m = a % 2
                    wait(pool, s_scr0, i, a)
                    wait_dma(pool, s_x, i, a)
                    wait(pool, s_x1, i, a - 1)
                    pool.tensor_tensor(base0[:, :], scr0[:, :], x_t[:, m, :], ALU.add).then_inc(s_base0, 1)
                if live(p, i):
                    m = p % 2
                    wait(pool, s_stat0, i, p)
                    pool.tensor_tensor(pw0[:, :], st0[:, m, 1:3], eps_one[:, :], ALU.add).then_inc(s_pe0, 1)
                    wait(pool, s_pe0, i, p)
                    wait(pool, s_x1, i, p - 2)
                    wait(pool, s_h0, i, p - 2)
                    pool.tensor_tensor(nm0[:, :], st0[:, m, 0:1], neg_one[:, :], ALU.mult)
                    pool.tensor_tensor(rd0[:, m, :], pw0[:, :], neg_half[:, :], ALU.pow).then_inc(s_pp0, 1)
                    wait(pool, s_pp0, i, p)
                    pool.tensor_tensor(sc0[:, m, 0:1], rd0[:, m, 0:1], rd0[:, m, 1:2], ALU.mult)\
                        .then_inc(s_pr0, 1)
                    wait(pool, s_pr0, i, p)
                    pool.tensor_tensor(sc0[:, m, 1:2], nm0[:, :], sc0[:, m, 0:1], ALU.mult).then_inc(s_ln0, 1)
                if live(c1, i):
                    m = c1 % 2
                    wait(pool, s_x1, i, c1)
                    wait(pool, s_xh, i, c1)
                    wait(pool, s_base2, i, c1 - 1)
                    pool.tensor_tensor(scr2[:, :], x1[:, m, :], xh[:, m, :], ALU.add).then_inc(s_psum2a, 1)
                    wait(pool, s_psum2a, i, c1)
                    pool.tensor_tensor(sum2[:, :], scr2[:, :], b2_all[:, :], ALU.add).then_inc(s_psum2b, 1)
                    wait(pool, s_stat2, i, c1)
                    pool.tensor_tensor(pw2[:, :], st2[:, 1:2], eps_one[:, 0:1], ALU.add).then_inc(s_pe2, 1)
                    pool.tensor_tensor(nm2[:, :], st2[:, 0:1], neg_one[:, :], ALU.mult)
                    wait(pool, s_pe2, i, c1)
                    pool.tensor_tensor(pz2[:, :], pw2[:, :], h_scale[:, :], ALU.mult).then_inc(s_pz2, 1)
                    wait(pool, s_pz2, i, c1)
                    wait(pool, s_hnh, i, c1 - 1)
                    wait(pool, s_hn, i, c1 - 1)
                    pool.tensor_tensor(sc2[:, 0:1], pz2[:, :], neg_half[:, 0:1], ALU.pow).then_inc(s_pp2, 1)
                    wait(pool, s_pp2, i, c1)
                    pool.tensor_tensor(sc2[:, 1:2], nm2[:, :], sc2[:, 0:1], ALU.mult).then_inc(s_ln2, 1)
                if live(a, i):
                    wait(pool, s_stat1, i, a)
                    pool.tensor_tensor(pw1[:, :], st1[:, 1:2], eps_one[:, 0:1], ALU.add).then_inc(s_pe1, 1)
                    pool.tensor_tensor(nm1[:, :], st1[:, 0:1], neg_one[:, :], ALU.mult)
                    wait(pool, s_pe1, i, a)
                    wait(pool, s_xh, i, a - 1)
                    pool.tensor_tensor(sc1[:, 0:1], pw1[:, :], neg_half[:, 0:1], ALU.pow).then_inc(s_pp1, 1)
                    wait(pool, s_pp1, i, a)
                    pool.tensor_tensor(sc1[:, 1:2], nm1[:, :], sc1[:, 0:1], ALU.mult).then_inc(s_ln1, 1)
                if live(c1, i):
                    m = c1 % 2
                    wait(pool, s_psum2b, i, c1)
                    wait(pool, s_vq, i, c1)
                    wait(pool, s_out, i, c1 - 2)
                    pool.tensor_tensor(base2[:, m, :], sum2[:, :], vq[:, :], ALU.add).then_inc(s_base2, 1)

            every_step(ENG.Pool, step)


def kernel(**inputs):
    import numpy as _np
    import concourse.bacc as _bacc
    from concourse import mybir as _mybir
    from concourse.bass_utils import run_bass_kernel_spmd as _run

    order = [
        ("x", inputs["x"]),
        ("adj", inputs["adj"]),
        ("W", inputs["L0_gnn_W"]),
        ("b", inputs["L0_gnn_b"]),
        ("W1T", _np.asarray(inputs["L1_gnn_W1"]).T),
        ("b1", inputs["L1_gnn_b1"]),
        ("gamma", _np.asarray(inputs["L1_gnn_gamma"]).reshape(-1, 128).T),
        ("beta", _np.asarray(inputs["L1_gnn_beta"]).reshape(-1, 128).T),
        ("W2T", _np.asarray(inputs["L1_gnn_W2"]).T),
        ("b2", inputs["L1_gnn_b2"]),
    ]
    nc = _bacc.Bacc("TRN2", target_bir_lowering=False, num_devices=1)
    arrays, args = {}, []
    for name, value in order:
        a = _np.ascontiguousarray(value)
        arrays[f"in_{name}_dram"] = a
        args.append(nc.dram_tensor(f"in_{name}_dram", a.shape, _mybir.dt.from_np(a.dtype), kind="ExternalInput").ap())
    shape = arrays["in_x_dram"].shape
    args.append(nc.dram_tensor("out_0_dram", shape, _mybir.dt.from_np(_np.dtype("float32")), kind="ExternalOutput").ap())
    bass_adjacency_prenorm_two_layer_gnn_kernel(nc, *args)
    r = _run(nc, [arrays], core_ids=[0])
    return r.results[0]["out_0_dram"]
```

```python
import concourse.bass as bass
from concourse import mybir
from contextlib import ExitStack


def bass_adjacency_prenorm_two_layer_gnn_kernel(
    nc: bass.Bass,
    x: bass.AP,
    adj: bass.AP,
    W: bass.AP,
    b: bass.AP,
    W1T: bass.AP,
    b1: bass.AP,
    gamma: bass.AP,
    beta: bass.AP,
    W2T: bass.AP,
    b2: bass.AP,
    out: bass.AP,
):
    F32, F32R, F16 = mybir.dt.float32, mybir.dt.float32r, mybir.dt.float16
    ALU = mybir.AluOpType
    ACT = mybir.ActivationFunctionType
    AX = mybir.AxisListType
    ENG = mybir.EngineType

    NG, N, DIN = x.shape
    DH = W1T.shape[1]
    CH = 512
    KI, KH = DIN // 128, DH // 128
    NCH = DH // CH
    EPS = 1e-5
    P_SCALE = 2.0 ** 8
    L_SCALE = 2.0 ** 8
    X_SCALE = 2.0 ** 11
    H_SCALE = 2.0 ** 10
    DN1_SCALE = 1.0 / (P_SCALE * X_SCALE)
    DN2_SCALE = 1.0 / (P_SCALE * H_SCALE)
    TINY = 1.1754944e-38
    SMALL = 5 * 16

    LOOP_FROM = 5
    LOOP_TO = NG - 1
    assert (LOOP_TO - LOOP_FROM) % 2 == 0 and LOOP_TO > LOOP_FROM
    ORDER = list(range(-1, LOOP_FROM)), list(range(LOOP_TO, NG + 3))

    ctx = ExitStack()
    with ctx:
        def sb(name, shape, dt=F32):
            return ctx.enter_context(nc.sbuf_tensor(name, shape, dt))

        def sem(name):
            return ctx.enter_context(nc.semaphore(name))

        stage = sb("stage", [128, 2, 4096])
        w0h, w0l = sb("w0h", [128, KI, DIN], F32R), sb("w0l", [128, KI, DIN], F32R)
        w1h, w1l = sb("w1h", [128, KI, DH], F32R), sb("w1l", [128, KI, DH], F32R)
        w2h, w2l = sb("w2h", [128, KH, DIN], F32R), sb("w2l", [128, KH, DIN], F32R)
        gam, bet = sb("gam", [128, KH]), sb("bet", [128, KH])
        bet_wide = sb("bet_wide", [128, KH, 128])
        b_all, b1_all, b2_all = sb("b_all", [128, DIN]), sb("b1_all", [128, DH]), sb("b2_all", [128, DIN])
        v_all = sb("v_all", [128, DIN])
        ident = sb("ident", [128, 128])
        neg_half = sb("neg_half", [128, 2])
        neg_one = sb("neg_one", [128, 1])
        ones = sb("ones", [128, 1], F16)
        ln0_scale = sb("ln0_scale", [128, 2])
        h_scale = sb("h_scale", [128, 1])
        eps_one = sb("eps_one", [128, 2])

        raw_w0 = stage[:, 0, 0:KI * DIN].rearrange("p (t n) -> p t n", t=KI)
        raw_w1 = stage[:, 1, :].rearrange("p (t n) -> p t n", t=KI)
        raw_w2 = stage[:, 0, :].rearrange("p (t n) -> p t n", t=KH)

        x_t = sb("x_t", [128, 2, DIN])
        adj_t = sb("adj_t", [128, 2, N])
        wrow_t = sb("wrow_t", [128, 2, N])
        hit = sb("hit", [128, N])
        diag_d = sb("diag_d", [128, N])
        adj_d = sb("adj_d", [128, N])
        ahat_T = sb("ahat_T", [128, N])
        L_hi, L_lo = sb("L_hi", [128, N], F16), sb("L_lo", [128, N], F16)
        H_T = sb("H_T", [128, 2, N], F16)
        HB_hi, HB_lo = sb("HB_hi", [128, 2, N], F16), sb("HB_lo", [128, 2, N], F16)
        P_hi, P_lo = sb("P_hi", [128, 2, N], F16), sb("P_lo", [128, 2, N], F16)
        h0 = sb("h0", [128, DIN])
        h0_hi, h0_lo = sb("h0_hi", [128, DIN], F16), sb("h0_lo", [128, DIN], F16)
        t0h, t0l = sb("t0h", [128, DIN], F32R), sb("t0l", [128, DIN], F32R)
        t1h, t1l = sb("t1h", [128, DIN], F32R), sb("t1l", [128, DIN], F32R)
        t2h, t2l = sb("t2h", [128, DH], F32R), sb("t2l", [128, DH], F32R)
        base0, scr0 = sb("base0", [128, DIN]), sb("scr0", [128, DIN])
        x1 = sb("x1", [128, 2, DIN])
        xh = sb("xh", [128, 2, DIN])
        xh_hi, xh_lo = sb("xh_hi", [128, DIN], F16), sb("xh_lo", [128, DIN], F16)
        z, h = sb("z", [128, DH]), sb("h", [128, DH])
        hn = sb("hn", [128, DH])
        hn_hi, hn_lo = sb("hn_hi", [128, DH], F16), sb("hn_lo", [128, DH], F16)
        sum2, scr2 = sb("sum2", [128, DIN]), sb("scr2", [128, DIN])
        vq = sb("vq", [128, DIN])
        base2 = sb("base2", [128, 2, DIN])
        out_t = sb("out_t", [128, 2, DIN])
        raw0, raw1, raw2 = sb("raw0", [128, 6]), sb("raw1", [128, 6]), sb("raw2", [128, NCH, 6])
        st0 = sb("st0", [128, 2, 3])
        st1, st2 = sb("st1", [128, 2]), sb("st2", [128, 2])
        pw0, pw1, pw2 = sb("pw0", [128, 2]), sb("pw1", [128, 1]), sb("pw2", [128, 1])
        pz0, pz2 = sb("pz0", [128, 2]), sb("pz2", [128, 1])
        rd0 = sb("rd0", [128, 2, 2])
        bias0 = sb("bias0", [128, 2, 1])
        sc1, sc2 = sb("sc1", [128, 2]), sb("sc2", [128, 2])
        nm0, nm1, nm2 = sb("nm0", [128, 1]), sb("nm1", [128, 1]), sb("nm2", [128, 1])
        qdn = sb("qdn", [128, 1])
        s_in = sb("s_in", [128, 1])
        deg, cnt = sb("deg", [128, 2]), sb("cnt", [128, 2])
        inv_b, inv_t = sb("inv_b", [128, 1]), sb("inv_t", [128, 1])
        inv_d, inv_r = sb("inv_d", [128, 1]), sb("inv_r", [128, 1])
        dn1, dn2 = sb("dn1", [128, 2]), sb("dn2", [128, 2])
        q = sb("q", [128, 2])

        def bank(name, n=1):
            return ctx.enter_context(nc.psum_tensor(name, [128, n * CH], F32))

        ps_t2 = bank("ps_t2", 2)
        ps_y1 = bank("ps_y1", 2)
        ps_t1 = bank("ps_t1")
        ps_t0 = bank("ps_t0")
        ps_at = bank("ps_at")
        ps_p = bank("ps_p")
        ps_y0 = ps_t1
        ps_y2 = ps_t2[:, 0:CH]
        ps_y2_last = ps_y0
        AT = ps_at[:, 0:N]
        ROW = ps_at[:, N:N + 1]
        PP = ps_p[:, 0:N]

        s_const = sem("consts_built")
        s_small = sem("small_params_loaded")
        s_stage = [sem("stage_loaded_0"), sem("stage_loaded_1")]
        s_w0h, s_w0l = sem("W_hi_blocks"), sem("W_lo_blocks")
        s_w1h, s_w1l = sem("W1_hi_blocks"), sem("W1_lo_blocks")
        s_w2h, s_w2l = sem("W2_hi_blocks"), sem("W2_lo_blocks")
        s_betw = sem("beta_widened")
        s_vps = sem("v_in_psum")
        s_v = sem("v_ready")
        s_x = [sem("x_loaded_0"), sem("x_loaded_1")]
        s_adj = [sem("adj_loaded_0"), sem("adj_loaded_1")]
        s_st = [sem("out_stored_0"), sem("out_stored_1")]
        s_zero = sem("ident_zeroed")
        s_diag, s_adjd, s_at, s_ht = sem("diag_D_ready"), sem("D_adj_ready"), sem("adjT_in_psum"), sem("HT_parts_ready")
        s_ahat, s_lth, s_lt = sem("ahatT_ready"), sem("LT_hi_ready"), sem("LT_lo_ready")
        s_stat0, s_ln0 = sem("stats0_ready"), sem("ln0_scalars_ready")
        s_h0, s_h0h, s_h0l = sem("h0_ready"), sem("h0_hi_ready"), sem("h0_lo_ready")
        s_t0, s_t0h, s_t0l = sem("t0_in_psum"), sem("t0_hi_ready"), sem("t0_lo_ready")
        s_s, s_scr0, s_base0 = sem("bias0_factor_ready"), sem("bias0_rows_ready"), sem("base0_ready")
        s_qdn, s_vq = sem("q_dn_product"), sem("beta_rows_ready")
        s_y0, s_x1 = sem("y0_in_psum"), sem("x1_ready")
        s_stat1, s_ln1, s_xh = sem("stats1_ready"), sem("ln1_scalars_ready"), sem("xh_ready")
        s_xhh, s_xhl = sem("xh_hi_ready"), sem("xh_lo_ready")
        s_p, s_ph, s_pl = sem("P_in_psum"), sem("P_hi_ready"), sem("P_lo_ready")
        s_t1, s_t1h, s_t1l = sem("t1_in_psum"), sem("t1_hi_ready"), sem("t1_lo_ready")
        s_y1 = [sem(f"y1_chunk{c}_in_psum") for c in range(NCH)]
        s_z = [sem(f"z_chunk{c}_ready") for c in range(NCH)]
        s_h = [sem(f"h_chunk{c}_ready") for c in range(NCH)]
        s_stat2, s_ln2, s_hn = sem("stats2_ready"), sem("ln2_scalars_ready"), sem("hn_ready")
        s_hnh, s_hnl = sem("hn_hi_ready"), sem("hn_lo_ready")
        s_dn2, s_base2 = sem("dn2_ready"), sem("base2_ready")
        s_t2, s_t2h, s_t2l = sem("t2_in_psum"), sem("t2_hi_ready"), sem("t2_lo_ready")
        s_y2, s_out = sem("y2_in_psum"), sem("out_ready")
        s_raw0, s_raw1, s_raw2 = sem("bn_raw0_ready"), sem("bn_raw1_ready"), sem("bn_raw2_ready")
        s_deg, s_degsafe, s_deginv, s_dn1 = sem("deg_ready"), sem("deg_safe"), sem("deg_inverted"), sem("dn1_ready")
        s_cnt, s_cntsafe, s_cntinv, s_hbhi = sem("cnt_ready"), sem("cnt_safe"), sem("cnt_inverted"), sem("HB_hi_ready")
        s_pe0, s_pz0, s_pp0 = sem("ln0_var_eps"), sem("ln0_var_scaled"), sem("ln0_rstd_and_D")
        s_pe1, s_pp1 = sem("ln1_var_eps"), sem("ln1_rstd")
        s_pe2, s_pz2, s_pp2 = sem("ln2_var_eps"), sem("ln2_var_scaled"), sem("ln2_rstd")
        s_psum2a, s_psum2b = sem("x1_plus_xh"), sem("x1_xh_b2_sum")

        def live(g, i):
            return not isinstance(i, int) or 0 <= g < NG

        def first_graph(i, g):
            return isinstance(i, int) and g == 0

        def last_graph(i, g):
            return isinstance(i, int) and g == NG - 1

        def wait(eng, s, i, g):
            if not isinstance(i, int) or g >= 0:
                eng.wait_ge(s, i + (g + 1))

        def wait_chunks(eng, s, i, g):
            eng.wait_ge(s, i * NCH + NCH * (g + 1))

        def wait_dma(eng, pair, i, g, each=16):
            if not isinstance(i, int) or g >= 0:
                eng.wait_ge(pair[g % 2], i * (each // 2) + each * (g // 2 + 1))

        def every_step(eng_type, step):
            for k in ORDER[0]:
                step(0, k)
            with nc.Fori(0, LOOP_TO - LOOP_FROM, 2, engines=(eng_type,), hint_back_edge=True) as i:
                step(i, LOOP_FROM)
                step(i, LOOP_FROM + 1)
            for k in ORDER[1]:
                step(0, k)

        block = ctx.enter_context(nc.Block())

        @block.sync
        def _(sp):
            def load_adj(i, g):
                n = g % 2
                at = bass.ds(i + g, 1)
                sp.dma_start(adj_t[:, n, :], adj[at, :, :].rearrange("g n e -> n (g e)")).then_inc(s_adj[n], 16)
                sp.dma_start(wrow_t[:, n, :], adj[at, 0, :].to_broadcast([128, N])).then_inc(s_adj[n], 16)

            def load_x(i, g):
                sp.dma_start(x_t[:, g % 2, :], x[bass.ds(i + g, 1), :, :].rearrange("g n f -> n (g f)"))\
                  .then_inc(s_x[g % 2], 16)

            load_adj(0, 0)
            load_x(0, 0)
            sp.dma_start(raw_w0, W.rearrange("(t p) n -> p t n", p=128)).then_inc(s_stage[0], 16)
            for row, src in ((b_all, b), (b1_all, b1), (b2_all, b2)):
                sp.dma_start(row[:, :], src.rearrange("(a n) -> a n", a=1).to_broadcast([128, src.shape[0]]))\
                  .then_inc(s_small, 16)
            for col, src in ((gam, gamma), (bet, beta)):
                sp.dma_start(col[:, :], src).then_inc(s_small, 16)
            load_adj(0, 1)
            load_x(0, 1)
            sp.dma_start(raw_w1, W1T.rearrange("(t p) n -> p t n", p=128)).then_inc(s_stage[1], 16)
            sp.wait_ge(s_w0h, KI)
            sp.wait_ge(s_w0l, KI)
            sp.dma_start(raw_w2, W2T.rearrange("(t p) n -> p t n", p=128)).then_inc(s_stage[0], 16)

            def step(i, k):
                g, o = k + 2, k - 3
                if live(o, i):
                    wait(sp, s_out, i, o)
                    sp.dma_start(out[bass.ds(i + o, 1), :, :].rearrange("g n f -> n (g f)"), out_t[:, o % 2, :])\
                      .then_inc(s_st[o % 2], 16)
                if isinstance(i, int) and not 2 <= g < NG:
                    return
                wait(sp, s_stat0, i, g - 2)
                wait(sp, s_adjd, i, g - 2)
                load_adj(i, g)
                wait(sp, s_h0, i, g - 2)
                wait(sp, s_base0, i, g - 2)
                load_x(i, g)

            for k in ORDER[0]:
                step(0, k)
            with nc.Fori(0, LOOP_TO - LOOP_FROM - 2, 2, engines=(ENG.SP,), hint_back_edge=True) as i:
                step(i, LOOP_FROM)
                step(i, LOOP_FROM + 1)
            for k in [LOOP_TO - 2, LOOP_TO - 1] + ORDER[1]:
                step(0, k)
            for g in (NG - 2, NG - 1):
                wait_dma(sp, s_st, 0, g)

        @block.tensor
        def _(pe):
            def thin(ps, lhs, rhs):
                (lh, ll), (rh, rl) = lhs, rhs
                pe.matmul(ps, lh, rh, start=True, stop=False)
                pe.matmul(ps, lh, rl, start=False, stop=False)
                return pe.matmul(ps, ll, rh, start=False, stop=True)

            def incidence_product(i, g):
                m = g % 2
                wait(pe, s_ht, i, g)
                wait(pe, s_pl, i, g - 1)
                pe.matmul(PP, HB_hi[:, m, :], H_T[:, m, :], start=True, stop=False)
                pe.matmul(PP, HB_lo[:, m, :], H_T[:, m, :], start=False, stop=True).then_inc(s_p, 1)

            def with_weights(ps, t_hi, t_lo, w_hi, w_lo, blocks, cols, low_ready,
                             first=None, between=None):
                for n, (t, w) in enumerate(((t_hi, w_hi), (t_hi, w_lo), (t_lo, w_hi))):
                    if n == 2:
                        low_ready()
                    for j in range(blocks):
                        if first is not None and n < 2:
                            pe.wait_ge(first[n], j + 1)
                        mm = pe.matmul(ps, t[:, j * 128:(j + 1) * 128], w[:, j, cols],
                                       start=(n == 0 and j == 0), stop=(n == 2 and j == blocks - 1))
                    if n == 0 and between is not None:
                        between()
                return mm

            def beta_row():
                pe.wait_ge(s_betw, 1)
                pe.wait_ge(s_stage[0], 32)
                for j in range(KH):
                    mm = pe.matmul(ps_y2, bet_wide[:, j, :], raw_w2[:, j, :], start=(j == 0), stop=(j == KH - 1))
                mm.then_inc(s_vps, 1)

            def step(i, k):
                p, a, c1, c2, o = k + 1, k, k - 1, k - 2, k - 3
                if live(a, i):
                    wait(pe, s_lt, i, a)
                    wait(pe, s_cnt, i, a)
                    wait(pe, s_h0h, i, a)
                    wait(pe, s_h0l, i, a)
                    wait(pe, s_t0l, i, a - 1)
                    pe.matmul(ROW, L_hi[:, :], ones[:, :], start=True, stop=False)
                    pe.matmul(ROW, L_lo[:, :], ones[:, :], start=False, stop=True)
                    for j in range(KI):
                        f = slice(j * 128, (j + 1) * 128)
                        mm = thin(ps_t0[:, f], (h0_hi[:, f], h0_lo[:, f]), (L_hi[:, :], L_lo[:, :]))
                    mm.then_inc(s_t0, 1)
                if live(c1, i):
                    m = c1 % 2
                    wait(pe, s_xhh, i, c1)
                    wait(pe, s_xhl, i, c1)
                    wait(pe, s_pl, i, c1)
                    wait(pe, s_x1, i, c1)
                    for j in range(KI):
                        f = slice(j * 128, (j + 1) * 128)
                        mm = thin(ps_t1[:, f], (xh_hi[:, f], xh_lo[:, f]), (P_hi[:, m, :], P_lo[:, m, :]))
                    mm.then_inc(s_t1, 1)
                if live(c2, i):
                    m = c2 % 2
                    wait(pe, s_hnh, i, c2)
                    wait(pe, s_hnl, i, c2)
                    wait(pe, s_t2l, i, c2 - 1)
                    if first_graph(i, c2):
                        pe.wait_ge(s_v, 1)
                    for j in [*range(KH // 2, KH), *range(KH // 2)]:
                        if j == 0:
                            wait(pe, s_out, i, o)
                        f = slice(j * 128, (j + 1) * 128)
                        mm = thin(ps_t2[:, f], (hn_hi[:, f], hn_lo[:, f]), (P_hi[:, m, :], P_lo[:, m, :]))
                    mm.then_inc(s_t2, 1)
                if live(c1, i):
                    wait(pe, s_t1h, i, c1)
                    for c in range(NCH):
                        wait(pe, s_z[c], i, c1 - 1)
                        cols = slice(c * CH, (c + 1) * CH)
                        with_weights(ps_y1[:, cols], t1h, t1l, w1h, w1l, KI, cols,
                                     low_ready=lambda: wait(pe, s_t1l, i, c1),
                                     first=(s_w1h, s_w1l) if first_graph(i, c1) else None).then_inc(s_y1[c], 1)
                if live(a, i):
                    wait(pe, s_t1l, i, c1)
                    wait(pe, s_t0h, i, a)
                    with_weights(ps_y0[:, :], t0h, t0l, w0h, w0l, KI, slice(0, DIN),
                                 low_ready=lambda: wait(pe, s_t0l, i, a),
                                 first=(s_w0h, s_w0l) if first_graph(i, a) else None).then_inc(s_y0, 1)
                if live(p, i):
                    wait(pe, s_s, i, a)
                    wait(pe, s_adjd, i, p)
                    pe.transpose(AT, adj_d[:, :], ident[:, :]).then_inc(s_at, 1)
                if live(a, i) and not live(c2, i):
                    incidence_product(i, a)
                if first_graph(i, c1):
                    beta_row()
                if live(c2, i):
                    wait(pe, s_t2h, i, c2)
                    last = last_graph(i, c2)
                    if not last:
                        wait(pe, s_t2l, i, c2)
                    with_weights(ps_y2_last[:, :] if last else ps_y2, t2h, t2l, w2h, w2l, KH, slice(0, DIN),
                                 low_ready=lambda: wait(pe, s_t2l, i, c2) if last else None,
                                 first=(s_w2h, s_w2l) if first_graph(i, c2) else None,
                                 between=(lambda: incidence_product(i, a)) if live(a, i) else None)\
                        .then_inc(s_y2, 1)

            every_step(ENG.PE, step)

        @block.scalar
        def _(act):
            def split_w0():
                act.wait_ge(s_stage[0], 16)
                for j in range(KI):
                    act.activation(w0h[:, j, :], raw_w0[:, j, :], ACT.Copy).then_inc(s_w0h, 1)

            def split_w1(blocks):
                act.wait_ge(s_stage[1], 16)
                for j in blocks:
                    act.activation(w1h[:, j, :], raw_w1[:, j, :], ACT.Copy).then_inc(s_w1h, 1)

            def split_w2(blocks):
                act.wait_ge(s_stage[0], 32)
                act.wait_ge(s_small, SMALL)
                for j in blocks:
                    act.activation(w2h[:, j, :], raw_w2[:, j, :], ACT.Copy, scale=gam[:, j:j + 1])\
                       .then_inc(s_w2h, 1)

            def beta_term(i, g):
                wait(act, s_qdn, i, g)
                if first_graph(i, g):
                    act.wait_ge(s_v, 1)
                wait(act, s_base2, i, g - 1)
                act.activation(vq[:, :], v_all[:, :], ACT.Copy, scale=qdn[:, :]).then_inc(s_vq, 1)

            def relu_chunk(i, g, c):
                cols = slice(c * CH, (c + 1) * CH)
                wait(act, s_z[c], i, g)
                act.activation(h[:, cols], z[:, cols], ACT.Relu).then_inc(s_h[c], 1)

            def step(i, k):
                p, a, c1, c2 = k + 1, k, k - 1, k - 2
                if first_graph(i, a):
                    split_w0()
                if live(c1, i):
                    wait(act, s_t1, i, c1)
                    wait(act, s_y1[NCH - 1], i, c1 - 1)
                    act.activation(t1h[:, :], ps_t1[:, :], ACT.Copy).then_inc(s_t1h, 1)
                if live(a, i):
                    wait(act, s_t0, i, a)
                    wait(act, s_y0, i, a - 1)
                    act.activation(t0h[:, :], ps_t0[:, :], ACT.Copy).then_inc(s_t0h, 1)
                if live(c2, i):
                    wait(act, s_t2, i, c2)
                    wait(act, s_y2, i, c2 - 1)
                    act.activation(t2h[:, :], ps_t2[:, :], ACT.Copy).then_inc(s_t2h, 1)
                if live(a, i):
                    wait(act, s_s, i, a)
                    if first_graph(i, a):
                        act.wait_ge(s_small, SMALL)
                    wait(act, s_base0, i, a - 1)
                    act.activation(scr0[:, :], b_all[:, :], ACT.Copy, scale=s_in[:, :]).then_inc(s_scr0, 1)
                if first_graph(i, c1):
                    split_w2(range(KH // 2))
                if live(c1, i):
                    if not first_graph(i, c1):
                        beta_term(i, c1)
                    wait(act, s_stat2, i, c1 - 1)
                    wait(act, s_hn, i, c1 - 1)
                    wait(act, s_hnh, i, c1 - 1)
                    relu_chunk(i, c1, 0)
                if live(c1, i):
                    for c in range(1, NCH):
                        relu_chunk(i, c1, c)
                if first_graph(i, a):
                    split_w1(range(KI // 2))
                if live(p, i):
                    m = p % 2
                    wait(act, s_ln0, i, p)
                    wait_dma(act, s_x, i, p)
                    wait(act, s_t0, i, p - 1)
                    act.activation(h0_hi[:, :], x_t[:, m, :], ACT.Relu, bias=bias0[:, m, :],
                                   scale=rd0[:, m, 0:1]).then_inc(s_h0h, 1)
                    wait(act, s_h0l, i, p - 1)
                    act.activation(h0[:, :], x_t[:, m, :], ACT.Relu, bias=bias0[:, m, :],
                                   scale=rd0[:, m, 0:1]).then_inc(s_h0, 1)
                if live(c1, i):
                    wait(act, s_ln2, i, c1)
                    wait(act, s_h[NCH - 1], i, c1)
                    wait(act, s_t2, i, c1 - 1)
                    act.activation(hn_hi[:, :], h[:, :], ACT.Identity, bias=sc2[:, 1:2],
                                   scale=sc2[:, 0:1]).then_inc(s_hnh, 1)
                if live(a, i):
                    m = a % 2
                    wait(act, s_p, i, a)
                    wait(act, s_t2, i, a - 2)
                    wait(act, s_base2, i, a - 2)
                    act.activation(P_hi[:, m, :], PP, ACT.Copy, accum_out=q[:, m:m + 1]).then_inc(s_ph, 1)
                if live(a, i):
                    m = a % 2
                    wait(act, s_ln1, i, a)
                    wait(act, s_base2, i, a - 2)
                    wait(act, s_xhl, i, a - 2)
                    act.activation(xh[:, m, :], x1[:, m, :], ACT.Relu, bias=sc1[:, 1:2],
                                   scale=sc1[:, 0:1]).then_inc(s_xh, 1)
                    wait(act, s_xh, i, a)
                    wait(act, s_t1, i, a - 1)
                    act.activation(xh_hi[:, :], xh[:, m, :], ACT.Copy, scale=X_SCALE).then_inc(s_xhh, 1)
                if first_graph(i, a):
                    split_w1(range(KI // 2, KI))
                if first_graph(i, c1):
                    split_w2(range(KH // 2, KH))
                    beta_term(i, c1)

            every_step(ENG.Activation, step)

        @block.vector
        def _(dve):
            def split_w0():
                for j in range(KI):
                    dve.wait_ge(s_w0h, j + 1)
                    dve.tensor_tensor(w0l[:, j, :], raw_w0[:, j, :], w0h[:, j, :].bitcast(F32), ALU.subtract)\
                       .then_inc(s_w0l, 1)

            def split_w1():
                for j in range(KI):
                    dve.wait_ge(s_w1h, j + 1)
                    dve.tensor_tensor(w1l[:, j, :], raw_w1[:, j, :], w1h[:, j, :].bitcast(F32), ALU.subtract)\
                       .then_inc(s_w1l, 1)

            def split_w2(blocks):
                for j in blocks:
                    dve.wait_ge(s_w2h, j + 1)
                    dve.scalar_tensor_tensor(out=w2l[:, j, :], in0=raw_w2[:, j, :], scalar=gam[:, j:j + 1],
                                             in1=w2h[:, j, :].bitcast(F32), op0=ALU.mult, op1=ALU.subtract)\
                       .then_inc(s_w2l, 1)

            def widen_beta():
                dve.wait_ge(s_small, SMALL)
                dve.tensor_copy(bet_wide[:, :, :], bet[:, :].unsqueeze(2).to_broadcast([128, KH, 128]))\
                   .then_inc(s_betw, 1)

            def scale_v():
                dve.wait_ge(s_vps, 1)
                dve.tensor_scalar(v_all[:, :], ps_y2, H_SCALE, None, ALU.mult).then_inc(s_v, 1)

            def stat2_chunk(i, g, c):
                wait(dve, s_h[c], i, g)
                dve.bn_stats(raw2[:, c, :], h[:, c * CH:(c + 1) * CH]).then_inc(s_raw2, 1)

            def step(i, k):
                p, a, c1, c2, o = k + 1, k, k - 1, k - 2, k - 3
                if live(o, i):
                    m = o % 2
                    y2 = ps_y2_last[:, :] if last_graph(i, o) else ps_y2
                    wait(dve, s_y2, i, o)
                    wait(dve, s_base2, i, o)
                    wait(dve, s_dn2, i, o)
                    wait_dma(dve, s_st, i, o - 2)
                    dve.scalar_tensor_tensor(out=out_t[:, m, :], in0=y2, scalar=dn2[:, m:m + 1],
                                             in1=base2[:, m, :], op0=ALU.mult, op1=ALU.add).then_inc(s_out, 1)
                if live(c1, i):
                    wait(dve, s_t1h, i, c1)
                    wait(dve, s_y1[NCH - 1], i, c1 - 1)
                    dve.tensor_tensor(t1l[:, :], ps_t1[:, :], t1h[:, :].bitcast(F32), ALU.subtract)\
                       .then_inc(s_t1l, 1)
                    m = c1 % 2
                    wait(dve, s_dn1, i, c1)
                    wait(dve, s_out, i, c1 - 2)
                    dve.tensor_scalar(dn2[:, m:m + 1], dn1[:, m:m + 1], DN2_SCALE / DN1_SCALE, None, ALU.mult)\
                       .then_inc(s_dn2, 1)
                    wait(dve, s_vq, i, c1 - 1)
                    wait(dve, s_ph, i, c1)
                    dve.scalar_tensor_tensor(out=qdn[:, :], in0=dn1[:, m:m + 1], scalar=DN2_SCALE / DN1_SCALE,
                                             in1=q[:, m:m + 1], op0=ALU.mult, op1=ALU.mult).then_inc(s_qdn, 1)
                if live(a, i):
                    wait(dve, s_t0, i, a)
                    wait(dve, s_scr0, i, a - 1)
                    dve.tensor_scalar(s_in[:, :], ROW, 1.0 / L_SCALE, None, ALU.mult).then_inc(s_s, 1)
                    wait(dve, s_t0h, i, a)
                    wait(dve, s_y0, i, a - 1)
                    dve.tensor_tensor(t0l[:, :], ps_t0[:, :], t0h[:, :].bitcast(F32), ALU.subtract)\
                       .then_inc(s_t0l, 1)
                    m = a % 2
                    wait(dve, s_cntinv, i, a)
                    dve.tensor_scalar(HB_hi[:, m, :], H_T[:, m, :], inv_t[:, :], None, ALU.mult)\
                       .then_inc(s_hbhi, 1)
                    wait(dve, s_hbhi, i, a)
                    dve.scalar_tensor_tensor(out=HB_lo[:, m, :], in0=H_T[:, m, :], scalar=inv_t[:, :],
                                             in1=HB_hi[:, m, :], op0=ALU.mult, op1=ALU.subtract)\
                       .then_inc(s_ht, 1)
                if first_graph(i, c2):
                    split_w2(range(KH - 2, KH))
                if live(c2, i):
                    wait(dve, s_t2h, i, c2)
                    wait(dve, s_y2, i, c2 - 1)
                    dve.tensor_tensor(t2l[:, :], ps_t2[:, :], t2h[:, :].bitcast(F32), ALU.subtract)\
                       .then_inc(s_t2l, 1)
                if live(p, i):
                    m = p % 2
                    wait_dma(dve, s_x, i, p)
                    dve.bn_stats(raw0[:, :], x_t[:, m, :]).then_inc(s_raw0, 1)
                    wait_dma(dve, s_adj, i, p, 32)
                    dve.scalar_tensor_tensor(out=hit[:, :], in0=adj_t[:, m, :], scalar=0.0, in1=wrow_t[:, m, :],
                                             op0=ALU.not_equal, op1=ALU.mult, accum_out=deg[:, m:m + 1])\
                       .then_inc(s_deg, 1)
                    wait(dve, s_ln0, i, p - 2)
                    wait(dve, s_raw0, i, p)
                    dve.reduce_sum(st0[:, m, 2:3], adj_t[:, m, :], AX.X)
                    dve.bn_aggr(st0[:, m, 0:2], raw0[:, :]).then_inc(s_stat0, 1)
                if first_graph(i, a):
                    split_w0()
                if first_graph(i, c1):
                    widen_beta()
                if live(c1, i):
                    m = c1 % 2
                    for c in range(NCH):
                        cols = slice(c * CH, (c + 1) * CH)
                        wait(dve, s_y1[c], i, c1)
                        wait(dve, s_h[c], i, c1 - 1)
                        dve.scalar_tensor_tensor(out=z[:, cols], in0=ps_y1[:, cols], scalar=dn1[:, m:m + 1],
                                                 in1=b1_all[:, cols], op0=ALU.mult, op1=ALU.add)\
                           .then_inc(s_z[c], 1)
                        if c < NCH - 1:
                            stat2_chunk(i, c1, c)
                    stat2_chunk(i, c1, NCH - 1)
                    wait_chunks(dve, s_raw2, i, c1)
                    wait(dve, s_ln2, i, c1 - 1)
                if live(a, i):
                    m = a % 2
                    wait(dve, s_deg, i, a)
                    dve.tensor_scalar(inv_d[:, :], deg[:, m:m + 1], TINY, 1.0 / DN1_SCALE, ALU.max, ALU.mult)\
                       .then_inc(s_degsafe, 1)
                if live(c1, i):
                    dve.bn_aggr(st2[:, :], raw2[:, :, :].rearrange("p c s -> p (c s)")).then_inc(s_stat2, 1)
                if live(a, i):
                    m = a % 2
                    wait(dve, s_y0, i, a)
                    wait(dve, s_base0, i, a)
                    wait(dve, s_base2, i, a - 2)
                    wait(dve, s_xh, i, a - 2)
                    dve.scalar_tensor_tensor(out=x1[:, m, :], in0=ps_y0[:, :], scalar=1.0 / (L_SCALE * X_SCALE),
                                             in1=base0[:, :], op0=ALU.mult, op1=ALU.add).then_inc(s_x1, 1)
                    wait(dve, s_x1, i, a)
                    dve.bn_stats(raw1[:, :], x1[:, m, :]).then_inc(s_raw1, 1)
                    wait(dve, s_raw1, i, a)
                    wait(dve, s_ln1, i, a - 1)
                    wait(dve, s_degsafe, i, a)
                    dve.reciprocal(inv_r[:, :], inv_d[:, :]).then_inc(s_deginv, 1)
                    dve.bn_aggr(st1[:, :], raw1[:, :]).then_inc(s_stat1, 1)
                if live(c1, i):
                    wait(dve, s_ln2, i, c1)
                    wait(dve, s_hnl, i, c1 - 1)
                    dve.tensor_scalar(hn[:, :], h[:, :], sc2[:, 0:1], sc2[:, 1:2], ALU.mult, ALU.add)\
                       .then_inc(s_hn, 1)
                if live(a, i):
                    m = a % 2
                    wait(dve, s_deginv, i, a)
                    dve.scalar_tensor_tensor(out=dn1[:, m:m + 1], in0=deg[:, m:m + 1], scalar=0.0,
                                             in1=inv_r[:, :], op0=ALU.is_gt, op1=ALU.mult).then_inc(s_dn1, 1)
                if live(p, i):
                    wait(dve, s_h0, i, p)
                    wait(dve, s_h0h, i, p)
                    wait(dve, s_t0, i, p - 1)
                    dve.tensor_tensor(h0_lo[:, :], h0[:, :], h0_hi[:, :], ALU.subtract).then_inc(s_h0l, 1)
                if live(a, i):
                    m = a % 2
                    wait(dve, s_ph, i, a)
                    wait(dve, s_t2, i, a - 2)
                    dve.tensor_tensor(P_lo[:, m, :], PP, P_hi[:, m, :], ALU.subtract).then_inc(s_pl, 1)
                if live(p, i):
                    m = p % 2
                    wait(dve, s_at, i, p)
                    wait(dve, s_diag, i, p)
                    wait(dve, s_lt, i, p - 1)
                    dve.tensor_tensor(ahat_T[:, :], AT, diag_d[:, :], ALU.add).then_inc(s_ahat, 1)
                    wait(dve, s_p, i, p - 2)
                    dve.tensor_scalar(H_T[:, m, :], AT, 0.0, None, ALU.not_equal, ALU.add,
                                      accum_out=cnt[:, m:m + 1]).then_inc(s_cnt, 1)
                    wait(dve, s_cnt, i, p)
                    dve.tensor_scalar(inv_b[:, :], cnt[:, m:m + 1], 1.0, 1.0 / P_SCALE, ALU.max, ALU.mult)\
                       .then_inc(s_cntsafe, 1)
                    wait(dve, s_ahat, i, p)
                    wait(dve, s_ln0, i, p)
                    wait(dve, s_t0, i, p - 1)
                    dve.tensor_scalar(L_hi[:, :], ahat_T[:, :], rd0[:, m, 1:2], None, ALU.mult).then_inc(s_lth, 1)
                    wait(dve, s_cntsafe, i, p)
                    dve.reciprocal(inv_t[:, :], inv_b[:, :]).then_inc(s_cntinv, 1)
                    wait(dve, s_lth, i, p)
                    dve.scalar_tensor_tensor(out=L_lo[:, :], in0=ahat_T[:, :], scalar=rd0[:, m, 1:2],
                                             in1=L_hi[:, :], op0=ALU.mult, op1=ALU.subtract).then_inc(s_lt, 1)
                if live(a, i):
                    m = a % 2
                    wait(dve, s_xhh, i, a)
                    wait(dve, s_t1, i, a - 1)
                    dve.scalar_tensor_tensor(out=xh_lo[:, :], in0=xh[:, m, :], scalar=X_SCALE, in1=xh_hi[:, :],
                                             op0=ALU.mult, op1=ALU.subtract).then_inc(s_xhl, 1)
                if live(c1, i):
                    wait(dve, s_hnh, i, c1)
                    wait(dve, s_hn, i, c1)
                    wait(dve, s_t2, i, c1 - 1)
                    dve.tensor_tensor(hn_lo[:, :], hn[:, :], hn_hi[:, :], ALU.subtract).then_inc(s_hnl, 1)
                if first_graph(i, a):
                    split_w1()
                if first_graph(i, c1):
                    scale_v()
                    split_w2(range(KH - 2))

            every_step(ENG.DVE, step)

        @block.gpsimd
        def _(pool):
            pool.memset(neg_half[:, :], -0.5)
            pool.memset(neg_one[:, :], -1.0)
            pool.memset(ones[:, :], 1.0)
            pool.memset(ln0_scale[:, 0:1], X_SCALE ** -2)
            pool.memset(ln0_scale[:, 1:2], 1.0 / L_SCALE)
            pool.memset(h_scale[:, :], H_SCALE ** -2)
            pool.memset(eps_one[:, 0:1], EPS)
            pool.memset(eps_one[:, 1:2], 1.0)
            pool.memset(ident[:, :], 0.0).then_inc(s_zero, 1)
            pool.wait_ge(s_zero, 1)
            pool.affine_select(out=ident[:, :], in_=ident[:, :], compare_op=ALU.not_equal, fill=1.0,
                               base=0, pattern=[[-1, 128]], channel_multiplier=1).then_inc(s_const, 1)
            pool.wait_ge(s_const, 1)

            def step(i, k):
                p, a, c1, o = k + 1, k, k - 1, k - 3
                if live(a, i):
                    m = a % 2
                    wait(pool, s_scr0, i, a)
                    wait_dma(pool, s_x, i, a)
                    wait(pool, s_x1, i, a - 1)
                    pool.tensor_tensor(base0[:, :], scr0[:, :], x_t[:, m, :], ALU.add).then_inc(s_base0, 1)
                if live(p, i):
                    m = p % 2
                    wait(pool, s_stat0, i, p)
                    pool.tensor_tensor(pw0[:, :], st0[:, m, 1:3], eps_one[:, :], ALU.add).then_inc(s_pe0, 1)
                    pool.tensor_tensor(nm0[:, :], st0[:, m, 0:1], neg_one[:, :], ALU.mult)
                    wait(pool, s_pe0, i, p)
                    pool.tensor_tensor(pz0[:, :], pw0[:, :], ln0_scale[:, :], ALU.mult).then_inc(s_pz0, 1)
                    wait(pool, s_pz0, i, p)
                    wait(pool, s_lt, i, p - 2)
                    wait(pool, s_h0, i, p - 2)
                    pool.tensor_tensor(rd0[:, m, :], pz0[:, :], neg_half[:, :], ALU.pow).then_inc(s_pp0, 1)
                    wait(pool, s_pp0, i, p)
                    pool.tensor_tensor(bias0[:, m, :], nm0[:, :], rd0[:, m, 0:1], ALU.mult).then_inc(s_ln0, 1)
                    wait_dma(pool, s_adj, i, p, 32)
                    wait(pool, s_at, i, p - 1)
                    pool.tensor_tensor(adj_d[:, :], adj_t[:, m, :], rd0[:, m, 1:2].to_broadcast([128, N]), ALU.mult)\
                        .then_inc(s_adjd, 1)
                    wait(pool, s_ahat, i, p - 1)
                    pool.tensor_tensor(diag_d[:, :], ident[:, :], rd0[:, m, 1:2].to_broadcast([128, N]), ALU.mult)\
                        .then_inc(s_diag, 1)
                if live(c1, i):
                    m = c1 % 2
                    wait(pool, s_x1, i, c1)
                    wait(pool, s_xh, i, c1)
                    wait(pool, s_base2, i, c1 - 1)
                    pool.tensor_tensor(scr2[:, :], x1[:, m, :], xh[:, m, :], ALU.add).then_inc(s_psum2a, 1)
                    wait(pool, s_stat2, i, c1)
                    pool.tensor_tensor(pw2[:, :], st2[:, 1:2], eps_one[:, 0:1], ALU.add).then_inc(s_pe2, 1)
                    pool.tensor_tensor(nm2[:, :], st2[:, 0:1], neg_one[:, :], ALU.mult)
                    wait(pool, s_pe2, i, c1)
                    pool.tensor_tensor(pz2[:, :], pw2[:, :], h_scale[:, :], ALU.mult).then_inc(s_pz2, 1)
                    wait(pool, s_pz2, i, c1)
                    wait(pool, s_hnh, i, c1 - 1)
                    wait(pool, s_hn, i, c1 - 1)
                    pool.tensor_tensor(sc2[:, 0:1], pz2[:, :], neg_half[:, 0:1], ALU.pow).then_inc(s_pp2, 1)
                    wait(pool, s_pp2, i, c1)
                    pool.tensor_tensor(sc2[:, 1:2], nm2[:, :], sc2[:, 0:1], ALU.mult).then_inc(s_ln2, 1)
                if live(a, i):
                    wait(pool, s_stat1, i, a)
                    pool.tensor_tensor(pw1[:, :], st1[:, 1:2], eps_one[:, 0:1], ALU.add).then_inc(s_pe1, 1)
                    pool.tensor_tensor(nm1[:, :], st1[:, 0:1], neg_one[:, :], ALU.mult)
                    wait(pool, s_pe1, i, a)
                    wait(pool, s_xh, i, a - 1)
                    pool.tensor_tensor(sc1[:, 0:1], pw1[:, :], neg_half[:, 0:1], ALU.pow).then_inc(s_pp1, 1)
                    wait(pool, s_pp1, i, a)
                    pool.tensor_tensor(sc1[:, 1:2], nm1[:, :], sc1[:, 0:1], ALU.mult).then_inc(s_ln1, 1)
                if live(c1, i):
                    m = c1 % 2
                    wait(pool, s_psum2a, i, c1)
                    pool.tensor_tensor(sum2[:, :], scr2[:, :], b2_all[:, :], ALU.add).then_inc(s_psum2b, 1)
                    wait(pool, s_psum2b, i, c1)
                    wait(pool, s_vq, i, c1)
                    wait(pool, s_out, i, c1 - 2)
                    pool.tensor_tensor(base2[:, m, :], sum2[:, :], vq[:, :], ALU.add).then_inc(s_base2, 1)

            every_step(ENG.Pool, step)


def kernel(**inputs):
    import numpy as _np
    import concourse.bacc as _bacc
    from concourse import mybir as _mybir
    from concourse.bass_utils import run_bass_kernel_spmd as _run

    order = [
        ("x", inputs["x"]),
        ("adj", inputs["adj"]),
        ("W", inputs["L0_gnn_W"]),
        ("b", inputs["L0_gnn_b"]),
        ("W1T", _np.asarray(inputs["L1_gnn_W1"]).T),
        ("b1", inputs["L1_gnn_b1"]),
        ("gamma", _np.asarray(inputs["L1_gnn_gamma"]).reshape(-1, 128).T),
        ("beta", _np.asarray(inputs["L1_gnn_beta"]).reshape(-1, 128).T),
        ("W2T", _np.asarray(inputs["L1_gnn_W2"]).T),
        ("b2", inputs["L1_gnn_b2"]),
    ]
    nc = _bacc.Bacc("TRN2", target_bir_lowering=False, num_devices=1)
    arrays, args = {}, []
    for name, value in order:
        a = _np.ascontiguousarray(value)
        arrays[f"in_{name}_dram"] = a
        args.append(nc.dram_tensor(f"in_{name}_dram", a.shape, _mybir.dt.from_np(a.dtype), kind="ExternalInput").ap())
    shape = arrays["in_x_dram"].shape
    args.append(nc.dram_tensor("out_0_dram", shape, _mybir.dt.from_np(_np.dtype("float32")), kind="ExternalOutput").ap())
    bass_adjacency_prenorm_two_layer_gnn_kernel(nc, *args)
    r = _run(nc, [arrays], core_ids=[0])
    return r.results[0]["out_0_dram"]
```
